# Optimizing a Trainium2 kernel written in Bass

```python
import numpy as np
import jax
import jax.numpy as jnp

def _softmax(x, axis=-1):
    return jax.nn.softmax(x, axis=axis)

def _gelu(x):
    return jax.nn.gelu(x, approximate=True)

def _silu(x):
    return jax.nn.silu(x)

def _sigmoid(x):
    return jax.nn.sigmoid(x)

def _layernorm(x, axis=-1, eps=1e-05):
    m = jnp.mean(x, axis=axis, keepdims=True)
    v = jnp.var(x, axis=axis, keepdims=True)
    return (x - m) / jnp.sqrt(v + eps)

def _scatter_add(tgt, idx, src, axis=0):
    return tgt.at[idx].add(src)

def _segment_sum(src, seg, n):
    return jax.ops.segment_sum(src, seg, n)
kernel_name = 'mk_conv_attn_hybrid_d2_conv_nhwc256_r2_33e697'

def setup_inputs(seed: int=0):
    np.random.seed(seed)
    _w = jnp.asarray

    def _rec_inputs():
        import jax
        import jax.numpy as jnp
        _gk = jax.random.key(seed)
        x = -0.000929 + 1 * jax.random.normal(jax.random.fold_in(_gk, 1), (4, 32, 32, 128), jnp.float32)
        return x
    x = _rec_inputs()

    def _L0_conv_setup():
        import jax, jax.numpy as jnp
        import numpy as np
        DIM = 128
        INNER = 256
        NH = 8
        DH = INNER // NH
        NB = INNER // 4
        BS = 4
        K = 4
        EPS = 1e-06
        LN_EPS = 1e-05

        def _mlstm_forward(x, W_up, conv_w, conv_b, Wq, Wk, Wv, W_i, b_i, W_f, b_f, norm_w, skip, W_down):
            B, H, W, C = x.shape
            S = H * W
            xs = x.reshape(B, S, C)
            up = xs @ W_up.T
            x_m, z = (up[..., :INNER], up[..., INNER:])
            xp = jnp.pad(x_m, ((0, 0), (K - 1, 0), (0, 0)))
            x_conv = conv_b + sum((xp[:, k:k + S, :] * conv_w[:, 0, k] for k in range(K)))
            x_act = jax.nn.silu(x_conv)
            xa = x_act.reshape(B, S, NB, BS)
            q = jnp.einsum('bsnd,nod->bsno', xa, Wq).reshape(B, S, INNER)
            k = jnp.einsum('bsnd,nod->bsno', xa, Wk).reshape(B, S, INNER)
            xv = x_m.reshape(B, S, NB, BS)
            v = jnp.einsum('bsnd,nod->bsno', xv, Wv).reshape(B, S, INNER)
            gate_in = jnp.concatenate([q, k, v], axis=-1)
            ig = (gate_in @ W_i.T + b_i).transpose(0, 2, 1)
            fg = (gate_in @ W_f.T + b_f).transpose(0, 2, 1)
            qh = q.reshape(B, S, NH, DH).transpose(0, 2, 1, 3)
            kh = k.reshape(B, S, NH, DH).transpose(0, 2, 1, 3) / np.sqrt(DH)
            vh = v.reshape(B, S, NH, DH).transpose(0, 2, 1, 3)
            lf = jax.nn.log_sigmoid(fg)
            lc = jnp.cumsum(lf, axis=-1)
            M = lc[..., :, None] - lc[..., None, :]
            mask = jnp.tril(jnp.ones((S, S), dtype=bool))
            logD = jnp.where(mask, M + ig[..., None, :], -jnp.inf)
            m = jnp.max(logD, axis=-1, keepdims=True)
            D = jnp.exp(logD - m)
            Cmat = jnp.einsum('bhid,bhjd->bhij', qh, kh) * D
            norm = jnp.maximum(jnp.abs(Cmat.sum(-1, keepdims=True)), jnp.exp(-m))
            h_cell = jnp.einsum('bhij,bhjd->bhid', Cmat / (norm + EPS), vh)
            mu = h_cell.mean(-1, keepdims=True)
            var = h_cell.var(-1, keepdims=True)
            hn = (h_cell - mu) / jnp.sqrt(var + LN_EPS)
            hn = hn * norm_w.reshape(NH, 1, DH)
            h = hn.transpose(0, 2, 1, 3).reshape(B, S, INNER)
            h = h + skip * x_act
            h = h * jax.nn.silu(z)
            out = h @ W_down.T
            return out.reshape(B, H, W, C)
        key = jax.random.key(seed)
        ks = jax.random.split(key, 14)
        f32 = jnp.float32
        return {'x': jax.random.normal(ks[0], (4, 32, 32, DIM), f32), 'W_up': jax.random.normal(ks[1], (2 * INNER, DIM), f32) * 0.05, 'conv_w': jax.random.normal(ks[2], (INNER, 1, K), f32) * 0.3, 'conv_b': jax.random.normal(ks[3], (INNER,), f32) * 0.05, 'Wq': jax.random.normal(ks[4], (NB, BS, BS), f32) * 0.3, 'Wk': jax.random.normal(ks[5], (NB, BS, BS), f32) * 0.3, 'Wv': jax.random.normal(ks[6], (NB, BS, BS), f32) * 0.3, 'W_i': jax.random.normal(ks[7], (NH, 3 * INNER), f32) * 0.02, 'b_i': jax.random.normal(ks[8], (NH,), f32) * 0.1, 'W_f': jax.random.normal(ks[9], (NH, 3 * INNER), f32) * 0.02, 'b_f': jax.random.normal(ks[10], (NH,), f32) * 0.1, 'norm_w': jnp.ones((INNER,), f32), 'skip': jax.random.normal(ks[11], (INNER,), f32) * 0.1, 'W_down': jax.random.normal(ks[12], (DIM, INNER), f32) * 0.05}
    _L0_conv_all = _L0_conv_setup()
    _L0_conv_in = {k: v for k, v in _L0_conv_all.items() if k in ('W_up', 'conv_w', 'conv_b', 'Wq', 'Wk', 'Wv', 'W_i', 'b_i', 'W_f', 'b_f', 'norm_w', 'skip', 'W_down')}
    del _L0_conv_all

    def _L1_attn_setup():
        import jax, jax.numpy as jnp
        import numpy as np
        T, N, D = (256, 512, 128)

        def _causal_attend(H, e):
            n = H.shape[1]
            m0 = jnp.full((n,), -jnp.inf, dtype=H.dtype)
            s0 = jnp.zeros((n,), dtype=H.dtype)
            num0 = jnp.zeros((n, H.shape[2]), dtype=H.dtype)

            def step(carry, inp):
                m, s, num = carry
                e_t, h_t = inp
                m_new = jnp.maximum(m, e_t)
                alpha = jnp.exp(m - m_new)
                p = jnp.exp(e_t - m_new)
                s_new = s * alpha + p
                num_new = num * alpha[:, None] + p[:, None] * h_t
                c_t = num_new / s_new[:, None]
                return ((m_new, s_new, num_new), c_t)
            _, C = jax.lax.scan(step, (m0, s0, num0), (e, H))
            return C
        key = jax.random.key(seed)
        k1, k2, k3, k4 = jax.random.split(key, 4)
        scale = 1.0 / np.sqrt(D)
        return {'H': jax.random.normal(k1, (T, N, D), dtype=jnp.float32), 'fc_w': jax.random.normal(k2, (D, D), dtype=jnp.float32) * scale, 'fc_b': jax.random.normal(k3, (D,), dtype=jnp.float32) * scale, 'score_w': jax.random.normal(k4, (D,), dtype=jnp.float32) * scale}
    _L1_attn_all = _L1_attn_setup()
    _L1_attn_in = {k: v for k, v in _L1_attn_all.items() if k in ('fc_w', 'fc_b', 'score_w')}
    del _L1_attn_all

    def _L1_ffn_setup():
        import jax, jax.numpy as jnp
        import numpy as np
        TOP_K = 2
        LN_EPS = 1e-05
        key = jax.random.key(seed)
        ks = jax.random.split(key, 8)
        B, S, D, E, H = (16, 512, 128, 8, 512)
        x = jax.random.normal(ks[0], (B, S, D), dtype=jnp.float32)
        Wr = jax.random.normal(ks[1], (D, E), dtype=jnp.float32) * 0.1
        br = jnp.zeros((E,), dtype=jnp.float32)
        ln_g = jnp.ones((E, D), dtype=jnp.float32)
        ln_b = jnp.zeros((E, D), dtype=jnp.float32)
        W1 = jax.random.normal(ks[2], (E, D, H), dtype=jnp.float32) * (1.0 / np.sqrt(D))
        b1 = jnp.zeros((E, H), dtype=jnp.float32)
        W2 = jax.random.normal(ks[3], (E, H, D), dtype=jnp.float32) * (1.0 / np.sqrt(H))
        b2 = jnp.zeros((E, D), dtype=jnp.float32)
        return {'x': x, 'Wr': Wr, 'br': br, 'ln_g': ln_g, 'ln_b': ln_b, 'W1': W1, 'b1': b1, 'W2': W2, 'b2': b2}
    _L1_ffn_all = _L1_ffn_setup()
    _L1_ffn_in = {k: v for k, v in _L1_ffn_all.items() if k in ('Wr', 'br', 'ln_g', 'ln_b', 'W1', 'b1', 'W2', 'b2')}
    del _L1_ffn_all
    return {'x': x, 'L0_conv_W_up': _L0_conv_in['W_up'], 'L0_conv_conv_w': _L0_conv_in['conv_w'], 'L0_conv_conv_b': _L0_conv_in['conv_b'], 'L0_conv_Wq': _L0_conv_in['Wq'], 'L0_conv_Wk': _L0_conv_in['Wk'], 'L0_conv_Wv': _L0_conv_in['Wv'], 'L0_conv_W_i': _L0_conv_in['W_i'], 'L0_conv_b_i': _L0_conv_in['b_i'], 'L0_conv_W_f': _L0_conv_in['W_f'], 'L0_conv_b_f': _L0_conv_in['b_f'], 'L0_conv_norm_w': _L0_conv_in['norm_w'], 'L0_conv_skip': _L0_conv_in['skip'], 'L0_conv_W_down': _L0_conv_in['W_down'], 'L1_attn_fc_w': _L1_attn_in['fc_w'], 'L1_attn_fc_b': _L1_attn_in['fc_b'], 'L1_attn_score_w': _L1_attn_in['score_w'], 'L1_ffn_Wr': _L1_ffn_in['Wr'], 'L1_ffn_br': _L1_ffn_in['br'], 'L1_ffn_ln_g': _L1_ffn_in['ln_g'], 'L1_ffn_ln_b': _L1_ffn_in['ln_b'], 'L1_ffn_W1': _L1_ffn_in['W1'], 'L1_ffn_b1': _L1_ffn_in['b1'], 'L1_ffn_W2': _L1_ffn_in['W2'], 'L1_ffn_b2': _L1_ffn_in['b2']}

def reference(x, L0_conv_W_up, L0_conv_conv_w, L0_conv_conv_b, L0_conv_Wq, L0_conv_Wk, L0_conv_Wv, L0_conv_W_i, L0_conv_b_i, L0_conv_W_f, L0_conv_b_f, L0_conv_norm_w, L0_conv_skip, L0_conv_W_down, L1_attn_fc_w, L1_attn_fc_b, L1_attn_score_w, L1_ffn_Wr, L1_ffn_br, L1_ffn_ln_g, L1_ffn_ln_b, L1_ffn_W1, L1_ffn_b1, L1_ffn_W2, L1_ffn_b2):
    import jax
    import jax.numpy as jnp

    def _L0_conv_ref(x, W_up, conv_w, conv_b, Wq, Wk, Wv, W_i, b_i, W_f, b_f, norm_w, skip, W_down):
        import jax, jax.numpy as jnp
        import numpy as np
        DIM = 128
        INNER = 256
        NH = 8
        DH = INNER // NH
        NB = INNER // 4
        BS = 4
        K = 4
        EPS = 1e-06
        LN_EPS = 1e-05

        def _mlstm_forward(x, W_up, conv_w, conv_b, Wq, Wk, Wv, W_i, b_i, W_f, b_f, norm_w, skip, W_down):
            B, H, W, C = x.shape
            S = H * W
            xs = x.reshape(B, S, C)
            up = xs @ W_up.T
            x_m, z = (up[..., :INNER], up[..., INNER:])
            xp = jnp.pad(x_m, ((0, 0), (K - 1, 0), (0, 0)))
            x_conv = conv_b + sum((xp[:, k:k + S, :] * conv_w[:, 0, k] for k in range(K)))
            x_act = jax.nn.silu(x_conv)
            xa = x_act.reshape(B, S, NB, BS)
            q = jnp.einsum('bsnd,nod->bsno', xa, Wq).reshape(B, S, INNER)
            k = jnp.einsum('bsnd,nod->bsno', xa, Wk).reshape(B, S, INNER)
            xv = x_m.reshape(B, S, NB, BS)
            v = jnp.einsum('bsnd,nod->bsno', xv, Wv).reshape(B, S, INNER)
            gate_in = jnp.concatenate([q, k, v], axis=-1)
            ig = (gate_in @ W_i.T + b_i).transpose(0, 2, 1)
            fg = (gate_in @ W_f.T + b_f).transpose(0, 2, 1)
            qh = q.reshape(B, S, NH, DH).transpose(0, 2, 1, 3)
            kh = k.reshape(B, S, NH, DH).transpose(0, 2, 1, 3) / np.sqrt(DH)
            vh = v.reshape(B, S, NH, DH).transpose(0, 2, 1, 3)
            lf = jax.nn.log_sigmoid(fg)
            lc = jnp.cumsum(lf, axis=-1)
            M = lc[..., :, None] - lc[..., None, :]
            mask = jnp.tril(jnp.ones((S, S), dtype=bool))
            logD = jnp.where(mask, M + ig[..., None, :], -jnp.inf)
            m = jnp.max(logD, axis=-1, keepdims=True)
            D = jnp.exp(logD - m)
            Cmat = jnp.einsum('bhid,bhjd->bhij', qh, kh) * D
            norm = jnp.maximum(jnp.abs(Cmat.sum(-1, keepdims=True)), jnp.exp(-m))
            h_cell = jnp.einsum('bhij,bhjd->bhid', Cmat / (norm + EPS), vh)
            mu = h_cell.mean(-1, keepdims=True)
            var = h_cell.var(-1, keepdims=True)
            hn = (h_cell - mu) / jnp.sqrt(var + LN_EPS)
            hn = hn * norm_w.reshape(NH, 1, DH)
            h = hn.transpose(0, 2, 1, 3).reshape(B, S, INNER)
            h = h + skip * x_act
            h = h * jax.nn.silu(z)
            out = h @ W_down.T
            return out.reshape(B, H, W, C)
        return _mlstm_forward(x, W_up, conv_w, conv_b, Wq, Wk, Wv, W_i, b_i, W_f, b_f, norm_w, skip, W_down)

    def _L1_attn_ref(H, fc_w, fc_b, score_w):
        import jax, jax.numpy as jnp
        import numpy as np
        T, N, D = (256, 512, 128)

        def _causal_attend(H, e):
            n = H.shape[1]
            m0 = jnp.full((n,), -jnp.inf, dtype=H.dtype)
            s0 = jnp.zeros((n,), dtype=H.dtype)
            num0 = jnp.zeros((n, H.shape[2]), dtype=H.dtype)

            def step(carry, inp):
                m, s, num = carry
                e_t, h_t = inp
                m_new = jnp.maximum(m, e_t)
                alpha = jnp.exp(m - m_new)
                p = jnp.exp(e_t - m_new)
                s_new = s * alpha + p
                num_new = num * alpha[:, None] + p[:, None] * h_t
                c_t = num_new / s_new[:, None]
                return ((m_new, s_new, num_new), c_t)
            _, C = jax.lax.scan(step, (m0, s0, num0), (e, H))
            return C
        Q = jnp.tanh(jnp.einsum('tnd,ed->tne', H, fc_w) + fc_b)
        e = jnp.einsum('tne,e->tn', Q, score_w)
        return _causal_attend(H, e)

    def _L1_ffn_ref(x, Wr, br, ln_g, ln_b, W1, b1, W2, b2):
        import jax, jax.numpy as jnp
        import numpy as np
        TOP_K = 2
        LN_EPS = 1e-05
        B, S, D = x.shape
        N = B * S
        xt = x.reshape(N, D)
        logits = xt @ Wr + br
        probs = jax.nn.softmax(logits, axis=-1)
        top_p, top_idx = jax.lax.top_k(probs, TOP_K)
        weights = top_p / top_p.sum(axis=-1, keepdims=True)
        mu = xt.mean(axis=-1, keepdims=True)
        var = ((xt - mu) ** 2).mean(axis=-1, keepdims=True)
        xn = (xt - mu) * jax.lax.rsqrt(var + LN_EPS)
        xe = xn[None, :, :] * ln_g[:, None, :] + ln_b[:, None, :]
        h = jax.nn.gelu(jnp.einsum('end,edh->enh', xe, W1) + b1[:, None, :], approximate=False)
        y = jnp.einsum('enh,ehd->end', h, W2) + b2[:, None, :]
        y_tok = jnp.transpose(y, (1, 0, 2))
        sel = jnp.take_along_axis(y_tok, top_idx[:, :, None], axis=1)
        out = (weights[:, :, None] * sel).sum(axis=1)
        return out.reshape(B, S, D)

    def _gn(v, G=32, eps=1e-05):
        B_, H_, W_, C_ = v.shape
        g = v.reshape(B_, H_, W_, G, C_ // G)
        m = jnp.mean(g, axis=(1, 2, 4), keepdims=True)
        s = jnp.var(g, axis=(1, 2, 4), keepdims=True)
        return ((g - m) / jnp.sqrt(s + eps)).reshape(v.shape)

    def _ln_c(v, eps=1e-06):
        m = jnp.mean(v, axis=-1, keepdims=True)
        s = jnp.var(v, axis=-1, keepdims=True)
        return (v - m) / jnp.sqrt(s + eps)

    def _ln_t(v, eps=1e-05):
        m = jnp.mean(v, axis=-1, keepdims=True)
        s = jnp.var(v, axis=-1, keepdims=True)
        return (v - m) / jnp.sqrt(s + eps)

    def _to_tokens(v):
        B_, H_, W_, C_ = v.shape
        return v.reshape(B_, H_ * W_, C_)

    def _from_tokens(t, like):
        return t.reshape(like.shape)
    x = x + _L0_conv_ref(_gn(x), L0_conv_W_up, L0_conv_conv_w, L0_conv_conv_b, L0_conv_Wq, L0_conv_Wk, L0_conv_Wv, L0_conv_W_i, L0_conv_b_i, L0_conv_W_f, L0_conv_b_f, L0_conv_norm_w, L0_conv_skip, L0_conv_W_down)
    t = _to_tokens(x)
    t = t + _L1_attn_ref(_ln_t(t), L1_attn_fc_w, L1_attn_fc_b, L1_attn_score_w)
    t = t + _L1_ffn_ref(_ln_t(t), L1_ffn_Wr, L1_ffn_br, L1_ffn_ln_g, L1_ffn_ln_b, L1_ffn_W1, L1_ffn_b1, L1_ffn_W2, L1_ffn_b2)
    x = _from_tokens(t, x)
    return x

_drawn_inputs = setup_inputs


def setup_inputs(seed=0):
    import zlib

    import numpy as np

    out = dict(_drawn_inputs(seed))
    spreads = {'L0_conv_norm_w': (1.0, 0.2),
     'L1_ffn_br': (0.0, 0.1),
     'L1_ffn_ln_g': (1.0, 0.2),
     'L1_ffn_ln_b': (0.0, 0.269),
     'L1_ffn_b1': (0.0, 0.1),
     'L1_ffn_b2': (0.0, 0.1)}
    factors = {'L0_conv_W_f': 3.547, 'L0_conv_b_f': 4.366, 'L0_conv_skip': 3.745, 'L1_attn_fc_b': 3.523}
    for name, (base, spread) in spreads.items():
        noise = np.random.default_rng([zlib.crc32(name.encode()), seed]).standard_normal(out[name].shape)
        drawn = base * np.exp(spread * noise) if base else spread * noise
        out[name] = jnp.asarray(drawn.astype(out[name].dtype))
    for name, factor in factors.items():
        out[name] = (out[name] * factor).astype(out[name].dtype)
    return out
```

```python
from contextlib import ExitStack

import concourse.bass as bass
from concourse import mybir

ALU = mybir.AluOpType
ACT = mybir.ActivationFunctionType
AX = mybir.AxisListType
F32 = mybir.dt.float32
BF16 = mybir.dt.bfloat16
I32 = mybir.dt.int32
U32 = mybir.dt.uint32

P = 128
B = 4
C = 128
S = 1024
T = S // P
N = B * P
TOK = B * S
INNER = 256
HALVES = INNER // P
NH = 8
DH = INNER // NH
HPH = NH // HALVES
DE = DH + 1
BH = B * NH
CONV = 4
E = 8
F = 512
FK = F // P
REGION = TOK + P
XW = C + 2
MOE_TILES = 2 * TOK // P + E
UNROLL = 4
SKIP = 1 << 20
NEG = -1.0e30
GN_EPS = 1e-5
LN_EPS = 1e-5
ROW_EPS = 1e-6


def bc(ap, axis, n):
    shape = list(ap.shape)
    shape.insert(axis, n)
    return ap.unsqueeze(axis).broadcast_to(shape)


class Ring:

    NEXT_X = ["xm0", "xm1"]
    NEXT_K = ["k0", "v0", "k1", "v1", "k2", "v2", "k3", "v3", "gateT", "q0", "q1", "kT0", "kT1"]
    NEXT_U = ["uq0", "uq1", "gtok"]
    ORDER = ([(n, "next") for n in NEXT_X]
             + [(n, "late") for n in ("y0", "y1", "down0", "down1", "hnT", "fc", "score")]
             + [("z0", "now"), ("z1", "now")] + [(n, "next") for n in NEXT_K]
             + [("tT", "late"), ("logit", "late")] + [(n, "next") for n in NEXT_U] + [("count", "late")])

    def __init__(self, prologue):
        self.names = {"first": self.pick("now", "next"), "middle": self.pick("now", "next", "late"),
                      "last": self.pick("now", "late"), "end": self.pick("late")}
        self.per = len(self.names["middle"])
        self.base = {"first": prologue, "middle": prologue + len(self.names["first"])}
        self.base["last"] = self.base["middle"] + (T - 2) * self.per
        self.base["end"] = self.base["last"] + len(self.names["last"])
        assert prologue % 2 == 0 and len(self.names["first"]) % 2 == 0 and self.per % 2 == 0

    def pick(self, *stages):
        return [n for n, stage in self.ORDER if stage in stages]

    def use(self, t, name):
        kind = {0: "first", T - 1: "last", T: "end"}.get(t, "middle") if isinstance(t, int) else "middle"
        n = self.base[kind] + self.names[kind].index(name)
        return n % 2, (n // 2 + (t - 1) * (self.per // 2) if kind == "middle" else n // 2)


def block_kernel(nc, a, out):
    ctx = ExitStack()
    with ctx:
        def sb(name, shape, dt=F32):
            return ctx.enter_context(nc.sbuf_tensor(name, shape, dt))

        def pb(name, shape, dt=F32):
            return ctx.enter_context(nc.psum_tensor(name, shape, dt))

        sems = {}

        def sem(name):
            if name not in sems:
                sems[name] = ctx.enter_context(nc.semaphore(name))
            return sems[name]

        xs = nc.dram_tensor("expert_rows", [E * REGION + P, XW], F32).ap()
        y2 = nc.dram_tensor("expert_out", [2 * TOK, C], F32).ap()
        x_d = a["x"].rearrange("b h w c -> b (h w) c")
        out_d = out.rearrange("b h w c -> b (h w) c")

        ident = sb("ident", [P, P])
        ident_b = sb("ident_b", [P, P], BF16)
        block4 = sb("block4", [P, P])
        avg4 = sb("avg4", [P, P])
        maskneg = sb("maskneg", [P, B, P], BF16)
        before = sb("before", [P, P], BF16)
        ones_b = sb("ones_b", [P, P], BF16)
        headmask = sb("headmask", [P, HPH, DE])
        pick = sb("pick", [96, NH, B], BF16)
        neghead = sb("neghead", [96, NH], BF16)
        ofbatch = sb("ofbatch", [96, B], BF16)
        spread = sb("spread", [BH, HALVES, B, HPH, DH])
        lower8 = sb("lower8", [P, E, E])
        mhalf = sb("mhalf", [P, N // P * 8])
        causal4 = sb("causal4", [P, B, B])
        region0 = sb("region0", [P, E])
        dest = sb("dest", [P, B, 2])
        tail = sb("tail", [P, XW])
        hsum = sb("hsum", [96, NH], BF16)
        iota8 = sb("iota8", [P, 8], I32)
        iotat = sb("iotat", [1, MOE_TILES], I32)

        wupT = sb("wupT", [C, 4, P])
        wdnT = sb("wdnT", [P, HALVES, C])
        fcwT = sb("fcwT", [C, C])
        wqkv_n = sb("wqkv_n", [P, 3, HALVES, 4])
        bd = sb("bd", [P, 3, HALVES, P])
        wgT = sb("wgT", [P, 6, 2 * NH])
        kg = sb("kg", [P, HALVES, P + 2 * NH])
        mg = sb("mg", [P, HALVES, 2 * NH])
        vecs = sb("vecs", [P, 3, HALVES])
        convw = sb("convw", [P, HALVES, CONV])
        fcb = sb("fcb", [C, 1])
        scw = sb("scw", [C, 1])
        bif = sb("bif", [BH, 2])
        wr = sb("wr", [C, E])
        brb = sb("brb", [P, E])
        lngbT = sb("lngbT", [C, 2 * E])
        w1 = sb("w1", [C, E, F])
        w2 = sb("w2", [P, E, FK, C])
        bias = sb("bias", [E, F + C])
        bias3 = sb("bias3", [3, E, F + C], BF16)
        lnbdiag = sb("lnbdiag", [C, E * E])

        x_tok = sb("x_tok", [P, B, T, C])
        xT = sb("xT", [C, B, S])
        gst = sb("gst", [C, B, 2, 6])
        gmv = sb("gmv", [C, B, 2])
        gm = sb("gm", [C, B])
        gd = sb("gd", [C, B])
        gv = sb("gv", [C, B])
        gr = sb("gr", [C, B])
        xm = sb("xm", [P, HALVES, B, CONV - 1 + P])
        cacc = sb("cacc", [P, HALVES, B, P])
        xact = sb("xact", [P, HALVES, B, P])
        sx = sb("sx", [P, HALVES, B, P])
        sz = sb("sz", [P, HALVES, B, P])
        qT = sb("qT", [P, HALVES, B, P])
        qpT = sb("qpT", [P, HALVES, B, P])
        kT = sb("kT", [P, HALVES, B, P])
        ktok = sb("ktok", [P, B, INNER])
        vext = sb("vext", [P, B, NH, DE])
        vs = sb("vs", [P, B, NH, DE])
        gates = sb("gates", [P, 2, B, NH])
        fabs = sb("fabs", [BH, P])
        fmin = sb("fmin", [BH, P])
        gpre = sb("gpre", [BH, 2, P])
        lcar = sb("lcar", [BH, 1])
        lc = sb("lc", [BH, P])
        gc = sb("gc", [BH, 2, P])
        rcar = sb("rcar", [BH, 2])
        r1 = sb("r1", [BH, 2, P])
        r2 = sb("r2", [BH, 2, P])
        gmid = sb("gmid", [BH, 2, P], BF16)
        parts = sb("parts", [96, 2, P], BF16)
        cexp = sb("cexp", [96, B, P], BF16)
        uq = sb("uq", [BH, P])
        gm2 = sb("gm2", [BH, 2, P])
        gtok = sb("gtok", [P, 2, B, NH])
        decay = sb("decay", [P, HALVES, B])
        D = sb("D", [P, 2, B, P])
        PT = sb("PT", [P, 2, B, P])
        KV = sb("KV", [P, HALVES * B, HPH * DE])
        KVm = sb("KVm", [P, HALVES * B, HPH * DE])
        osb = sb("osb", [P, 2, B, HPH, DE])
        nrm = sb("nrm", [P, 2, B, HPH])
        rr = sb("rr", [P, 2, B, HPH])
        mu = sb("mu", [P, 2, B, HPH])
        dd = sb("dd", [P, 2, B, HPH, DH])
        dsq = sb("dsq", [P, 2, B, HPH, DH])
        var = sb("var", [P, 2, B, HPH])
        hn = sb("hn", [P, B, NH, DH])
        yT = sb("yT", [P, HALVES, B, P])
        x1 = sb("x1", [P, B, C])
        st1 = sb("st1", [P, B, 6])
        mv1 = sb("mv1", [P, B, 2])
        rs1 = sb("rs1", [P, B])
        hnm = sb("hnm", [P, B, C])
        hnmT = sb("hnmT", [C, B, P])
        qat = sb("qat", [C, B, P])
        esc = sb("esc", [P, B])
        emax = sb("emax", [P, B])
        wat = sb("wat", [P, B, B])
        wsum = sb("wsum", [P, B])
        st3 = sb("st3", [P, B, 6])
        mv3 = sb("mv3", [P, B, 2])
        rs3 = sb("rs3", [P, B])
        v2 = sb("v2", [P, B])
        rs4 = sb("rs4", [P, B])
        xt = sb("xt", [P, B, C])
        xtT = sb("xtT", [C, B, P])
        lg = sb("lg", [P, B, E])
        lmax = sb("lmax", [P, B])
        cmp = sb("cmp", [P, B, E, E])
        ceq = sb("ceq", [P, B, E, E])
        rank = sb("rank", [P, B, E])
        oh = sb("oh", [P, 2, B, E])
        selb = sb("selb", [P, B, E], BF16)
        pex = sb("pex", [P, B, E])
        wk = sb("wk", [P, 2, B])
        wks = sb("wks", [P, B])
        tmpk = sb("tmpk", [P, 2, B, E])
        pos = sb("pos", [P, B, E])
        offs = sb("offs", [P, E])
        slotf = sb("slotf", [P, 2, B])
        slot = sb("slot", [P, 2, B], I32)
        xrow = sb("xrow", [P, B, 2, XW])

        cnt = sb("cnt", [1, E])
        tls = sb("tls", [1, E])
        tlsi = sb("tlsi", [1, E], I32)
        tend = sb("tend", [1, E])
        tbeg = sb("tbeg", [1, E])
        eones = sb("eones", [1, E])
        til = sb("til", [1, MOE_TILES])
        tef = sb("tef", [1, MOE_TILES])
        trf = sb("trf", [1, MOE_TILES])
        table = sb("table", [1, 2, MOE_TILES], I32)
        tailrow = sb("tailrow", [1, E], I32)

        def over(buf, lo, *shape):
            flat = buf[:] if len(buf.shape) == 2 else buf[:].rearrange(
                {3: "p a b -> p (a b)", 4: "p a b c -> p (a b c)", 5: "p a b c d -> p (a b c d)"}[len(buf.shape)])
            n = 1
            for d in shape[1:]:
                n *= d
            v = flat[0:shape[0], lo:lo + n]
            if len(shape) == 3:
                return v.rearrange("p (a b) -> p a b", a=shape[1])
            if len(shape) == 4:
                return v.rearrange("p (a b c) -> p a b c", a=shape[1], b=shape[2])
            return v

        wup_n = over(hn, 0, P, 4, C)
        wdn_n = over(hn, 4 * C, C, INNER)
        fcw_n = over(hn, 4 * C + INNER, C, C)
        bdT = over(dd, 0, P, 3, HALVES, P)
        wg_n = over(dsq, 0, 2 * NH, 3 * INNER)
        lngb_n = over(dsq, 3 * INNER, 2 * E, C)
        bparts = over(xrow.bitcast(BF16), 0, E, 3, F + C)
        past = over(qT, 0, 1, MOE_TILES, E)
        ina = over(kT, 0, 1, MOE_TILES, E)
        rowt = over(cacc, 0, 1, MOE_TILES, E)
        xin = over(vs, 0, P, 2 * UNROLL, XW)
        hid = over(sz, 0, P, 2, F)
        hidT = over(sx, 0, P, 2, FK, P)
        yout = over(yT, 0, P, UNROLL, C)
        xeT = over(yT, UNROLL * C, C, 2, P)
        ya = xT[:, :, :].rearrange("p b (i k c) -> p i k b c", i=4, k=2)

        pG = [pb(f"pG{i}", [P, 512]) for i in range(2)]
        pA = [pb(f"pA{i}", [P, 512]) for i in range(2)]
        pS = [pb(f"pS{i}", [P, 512]) for i in range(2)]
        pO = [pb(f"pO{i}", [P, 512]) for i in range(2)]

        PRO = ([f"x{i}" for i in range(8)] + ["wup", "wdn", "fcw", "bd0", "bd1", "gate", "lnT"]
               + ["gmean", "gvar", "geffx", "geffm"] + ["b1"]
               + Ring.NEXT_X + Ring.NEXT_K + Ring.NEXT_U)
        ring = Ring(len(PRO))

        def use(t, name):
            if t is None:
                n = PRO.index(name)
                return n % 2, n // 2
            return ring.use(t, name)

        def claim(eng, t, name):
            bank, n = use(t, name)
            if not (isinstance(n, int) and n == 0):
                eng.wait_ge(sem(f"general{bank}_read"), n)
            return pG[bank], sem(f"general{bank}_written")

        def arrived(eng, t, name):
            bank, n = use(t, name)
            eng.wait_ge(sem(f"general{bank}_written"), n + 1)
            return pG[bank], sem(f"general{bank}_read")

        def taken(eng, t, name):
            bank, n = use(t, name)
            eng.wait_ge(sem(f"general{bank}_read"), n + 1)

        def wait_apart(eng, semaphore, value):
            eng.wait_ge(semaphore, value)
            if not isinstance(value, int):
                eng.sem_inc(sem("waits_apart"), 1)

        block = ctx.enter_context(nc.Block())

        def between(eng, step):
            step(0)
            with eng.Fori(1, T - 1) as t:
                step(t)
            step(T - 1)

        @block.sync
        def _(sp):
            for b in range(B):
                for h in range(2):
                    sp.dma_start(x_tok[:, b, 4 * h:4 * h + 4, :],
                                 x_d[b, 512 * h:512 * h + 512, :].rearrange("(t p) c -> p t c", p=P)
                                 ).then_inc(sem(f"x_loaded{b}{h}"), 16)
            sp.dma_start(w1[:, :, :], a["L1_ffn_W1"].rearrange("e d f -> d e f")).then_inc(sem("w1_loaded"), 16)
            for e in range(E):
                sp.dma_start(w2[:, e, :, :], a["L1_ffn_W2"][e].rearrange("(k p) d -> p k d", p=P)
                             ).then_inc(sem("w2_loaded"), 16)

            sp.wait_ge(sem("bparts_made"), 1)
            for k in range(3):
                sp.dma_start(bias3[k:k + 1, :, :], bparts[:, k:k + 1, :]
                             ).then_inc(sem("bias3_made"), 16)

            sp.wait_ge(sem("tails_known"), 1)
            sp.wait_ge(sem("pool_tables_made"), 1)
            for k in range(2):
                for b in range(B):
                    sp.wait_ge(sem(f"scattered{k}{b}"), 16 * T)
            for e in range(E):
                row = sp.value_load(tailrow[0:1, e:e + 1], min_val=0, max_val=E * REGION - P)
                sp.dma_start(xs[bass.ds(row, P), :], tail[:, :]).then_inc(sem("tails_written"), 16)
            sp.dma_start(xs[E * REGION:E * REGION + P, :], tail[:, :]).then_inc(sem("tails_written"), 16)
            sp.wait_ge(sem("tails_written"), 16 * (E + 1))
            sp.wait_ge(sem("table_made"), 1)

            def load(i, u):
                row = sp.value_load(table[0:1, 1, bass.ds(i, 1)], min_val=0, max_val=E * REGION)
                sp.dma_start(xin[:, u, :], xs[bass.ds(row, P), :]).then_inc(sem(f"rows_loaded{u}"), 16)

            for u in range(2 * UNROLL):
                load(u, u)
            with sp.Fori(1, MOE_TILES // (2 * UNROLL)) as r:
                for u in range(2 * UNROLL):
                    sp.wait_ge(sem(f"y_sent{u}"), 16 * r)
                    load(r * 2 * UNROLL + u, u)

            for u in range(2 * UNROLL):
                sp.wait_ge(sem(f"y_sent{u}"), 16 * (MOE_TILES // (2 * UNROLL)))
            for t in range(T):
                if t >= 4:
                    sp.wait_ge(sem("sum_done"), t - 3)
                for k in range(2):
                    sp.dma_start(ya[:, t % 4, k, :, :],
                                 y2[k * TOK:(k + 1) * TOK, :].rearrange("(b t p) c -> t p b c", b=B, p=P)[t]
                                 ).then_inc(sem(f"y_loaded{t % 4}"), 16)

        @block.scalar
        def _(act):
            def g(src, pat=None, **kw):
                return a[src].rearrange(pat, **kw) if pat else a[src]

            with nc.allow_non_contiguous_dma(reason="small weights, once"):
                for dst, src in [
                    (wup_n[:, :, :], g("L0_conv_W_up", "(o p) c -> p o c", p=P)),
                    (wdn_n[:, :], g("L0_conv_W_down")),
                    (fcw_n[:, :], g("L1_attn_fc_w")),
                    (wqkv_n[:, 0], g("L0_conv_Wq", "(f n) o d -> (n o) f d", f=HALVES)),
                    (wqkv_n[:, 1], g("L0_conv_Wk", "(f n) o d -> (n o) f d", f=HALVES)),
                    (wqkv_n[:, 2], g("L0_conv_Wv", "(f n) o d -> (n o) f d", f=HALVES)),
                    (wg_n[0:NH, :], g("L0_conv_W_i")),
                    (wg_n[NH:2 * NH, :], g("L0_conv_W_f")),
                    (vecs[:, 0], g("L0_conv_conv_b", "(f p) -> p f", p=P)),
                    (vecs[:, 1], g("L0_conv_norm_w", "(f p) -> p f", p=P)),
                    (vecs[:, 2], g("L0_conv_skip", "(f p) -> p f", p=P)),
                    (convw[:, :, :], g("L0_conv_conv_w", "(f p) a k -> p f (a k)", p=P)),
                    (fcb[:, :], g("L1_attn_fc_b", "(p a) -> p a", a=1)),
                    (scw[:, :], g("L1_attn_score_w", "(p a) -> p a", a=1)),
                    (wr[:, :], g("L1_ffn_Wr")),
                    (brb[:, :], g("L1_ffn_br", "(a e) -> a e", a=1).broadcast_to([P, E])),
                    (lngb_n[0:E, :], g("L1_ffn_ln_g")),
                    (lngb_n[E:2 * E, :], g("L1_ffn_ln_b")),
                    (bias[:, 0:F], g("L1_ffn_b1")),
                    (bias[:, F:F + C], g("L1_ffn_b2")),
                ] + [(bif[NH * b:NH * b + NH, k:k + 1], g(("L0_conv_b_i", "L0_conv_b_f")[k], "(h a) -> h a", a=1))
                     for b in range(B) for k in range(2)]:
                    act.dma_start(dst, src).then_inc(sem("weights_loaded"), 16)

            for i in range(8):
                bank, read = arrived(act, None, f"x{i}")
                nc.scalar.activation(xT[:, i // 2, 512 * (i % 2):512 * (i % 2) + 512], bank[:, :],
                                     ACT.Copy).then_inc(read, 1)
            bank, read = arrived(act, None, "wup")
            nc.scalar.activation(wupT[:, :, :].rearrange("p o c -> p (o c)"), bank[:, :], ACT.Copy).then_inc(read, 1)
            bank, read = arrived(act, None, "wdn")
            nc.scalar.activation(wdnT[:, :, :].rearrange("p o c -> p (o c)"), bank[:, 0:256],
                                 ACT.Copy).then_inc(read, 1)
            bank, read = arrived(act, None, "fcw")
            nc.scalar.activation(fcwT[:, :], bank[:, 0:C], ACT.Copy).then_inc(read, 1)

            def silu_x(t):
                for f in range(HALVES):
                    act.wait_ge(sem("conv_done"), 2 * t + f + 1)
                    nc.scalar.activation(xact[:, f], cacc[:, f], ACT.Silu).then_inc(sem("xact_ready"), 1)

            def xm_copy(t, src):
                for f in range(HALVES):
                    bank, read = arrived(act, src, f"xm{f}")
                    act.wait_ge(sem("halo_moved"), 2 * t + f + 1)
                    nc.scalar.activation(xm[:, f, :, CONV - 1:], bank[:, :].rearrange("p (b i) -> p b i", b=B),
                                         ACT.Copy).then_inc(read, 1)

            def qkv(t, src):
                for b in range(B):
                    bank, read = arrived(act, src, f"k{b}")
                    if b == 0 and not (isinstance(t, int) and t == 0):
                        act.wait_ge(sem("state_summed"), t)
                    nc.scalar.activation(ktok[:, b, :].rearrange("p (f c) -> p f c", f=2),
                                         bank[:, 0:2 * (P + 16)].rearrange("p (f c) -> p f c", f=2)[:, :, 0:P],
                                         ACT.Copy).then_inc(sem("ktok_part"), 1)
                    nc.scalar.activation(gates[:, :, b, :],
                                         bank[:, P:P + 16].rearrange("p (k h) -> p k h", k=2),
                                         ACT.Copy).then_inc(read, 1)
                    bank, read = arrived(act, src, f"v{b}")
                    nc.scalar.activation(vext[:, b, :, 0:DH], bank[:, 0:INNER].rearrange("p (h d) -> p h d", h=NH),
                                         ACT.Copy).then_inc(read, 1)

            def qkv2(t, src):
                bank, read = arrived(act, src, "gateT")
                nc.scalar.activation(fabs[:, :], bank[0:BH, P:2 * P], ACT.Abs, bias=bif[:, 1:2]
                                     ).then_inc(sem("fabs_done"), 1)
                for k in range(2):
                    ins = nc.scalar.activation(gpre[:, k, :], bank[0:BH, P * k:P * k + P], ACT.Identity,
                                               bias=bif[:, k:k + 1])
                    ins.then_inc(*((sem("gpre_i_ready"), 1) if k == 0 else (read, 1)))
                act.wait_ge(sem("fabs_done"), t + 1)
                nc.scalar.activation(fabs[:, :], fabs[:, :], ACT.Exp, scale=-1.0).then_inc(sem("fexp_done"), 1)
                act.wait_ge(sem("fexp_done"), t + 1)
                nc.scalar.activation(fabs[:, :], fabs[:, :], ACT.Ln, bias=1.0).then_inc(sem("fln_done"), 1)
                for n, (name, dst) in enumerate([("q0", qT[:, 0]), ("q1", qT[:, 1]), ("kT0", kT[:, 0]), ("kT1", kT[:, 1])]):
                    bank, read = arrived(act, src, name)
                    nc.scalar.activation(dst.rearrange("p b i -> p (b i)"), bank[:, :], ACT.Copy,
                                         scale=DH ** -0.5 if n < 2 else 1.0).then_inc(read, 1)

            def qkv3(t, src):
                act.wait_ge(sem("c_ready"), t + 1)
                nc.scalar.activation(uq[:, :], gc[:, 1, :], ACT.Exp, bias=rcar[:, 0:1], scale=-1.0
                                     ).then_inc(sem("uq_ready"), 1)
                act.wait_ge(sem("r_end_ready"), t + 1)
                nc.scalar.activation(gm2[:, 0, :], gc[:, 0, :], ACT.Exp, bias=rcar[:, 1:2]
                                     ).then_inc(sem("gm2_done"), 1)
                act.wait_ge(sem("m_ready"), t + 1)
                nc.scalar.activation(gm2[:, 1, :], fmin[:, :], ACT.Exp, scale=-1.0).then_inc(sem("gm2_done"), 1)
                bank, read = arrived(act, src, "gtok")
                if not (isinstance(t, int) and t == 0):
                    act.wait_ge(sem("norm_taken"), 2 * t)
                nc.scalar.activation(gtok[:, 0].rearrange("p b h -> p (b h)"), bank[:, 0:BH],
                                     ACT.Copy).then_inc(sem("gscale_ready"), 1)
                nc.scalar.activation(gtok[:, 1].rearrange("p b h -> p (b h)"), bank[:, BH:2 * BH],
                                     ACT.Copy).then_inc(read, 1)

            def exps(t, h):
                act.wait_ge(sem("exponents_ready"), NH * t + h + 1)
                if not (isinstance(t, int) and t == 0 and h < 2):
                    act.wait_ge(sem("weighted"), NH * t + h - 1)
                nc.scalar.activation(D[:, h % 2].rearrange("p b i -> p (b i)"), pA[h % 2][:, :], ACT.Exp
                                     ).then_inc(sem("decay_ready"), 1)

            def out_copy(t, f):
                act.wait_ge(sem("half_ready"), 2 * t + f + 1)
                if not (isinstance(t, int) and t == 0):
                    act.wait_ge(sem("norm_read"), 2 * t + f - 1)
                for k in range(2):
                    nc.scalar.activation(osb[:, f, 2 * k:2 * k + 2].rearrange("p b h d -> p (b h d)"),
                                         pO[k][:, 0:2 * HPH * DE], ACT.Copy).then_inc(sem("half_copied"), 1)

            def attn1(t, s):
                bank, read = arrived(act, t, "hnT")
                nc.scalar.activation(hnmT[:, :, :].rearrange("p b i -> p (b i)"), bank[:, :], ACT.Copy
                                     ).then_inc(read, 1)

            def attn1b(t, s):
                bank, read = arrived(act, t, "fc")
                nc.scalar.activation(qat[:, :, :].rearrange("p b i -> p (b i)"), bank[:, :], ACT.Tanh,
                                     bias=fcb[:, 0:1]).then_inc(read, 1)

            def attn2(t, s):
                act.wait_ge(sem("wat_ready"), s + 1)
                nc.scalar.activation(wat[:, :, :], wat[:, :, :], ACT.Exp).then_inc(sem("wat_exp"), 1)

            def attn3(t, s):
                bank, read = arrived(act, t, "tT")
                nc.scalar.activation(xtT[:, :, :].rearrange("p b i -> p (b i)"), bank[:, :], ACT.Copy
                                     ).then_inc(read, 1)

            def attn4(t, s):
                act.wait_ge(sem("pex_ready"), s + 1)
                nc.scalar.activation(pex[:, :, :], pex[:, :, :], ACT.Exp).then_inc(sem("pex_exp"), 1)

            xm_copy(0, None)
            silu_x(0)
            qkv(0, None)
            qkv2(0, None)
            qkv3(0, None)

            def silu_z(t):
                for f in range(HALVES):
                    bank, read = arrived(act, t, f"z{f}")
                    nc.scalar.activation(sz[:, f].rearrange("p b i -> p (b i)"), bank[:, :], ACT.Silu
                                         ).then_inc(read, 1)

            def step(t):
                first, last = (isinstance(t, int) and t == 0), (isinstance(t, int) and t == T - 1)
                exps(t, 0)
                if not last:
                    xm_copy(t + 1, t)
                for h in range(1, 4):
                    exps(t, h)
                out_copy(t, 0)
                exps(t, 4)
                exps(t, 5)
                if not first:
                    attn1(t, t - 1)
                exps(t, 6)
                if not first:
                    attn1b(t, t - 1)
                exps(t, 7)
                if not last:
                    act.wait_ge(sem("sx_ready"), t + 1)
                    silu_x(t + 1)
                silu_z(t)
                if not first:
                    attn2(t, t - 1)
                out_copy(t, 1)
                if not last:
                    qkv(t + 1, t)
                    qkv2(t + 1, t)
                if not first:
                    attn3(t, t - 1)
                if not last:
                    qkv3(t + 1, t)
                if not first:
                    attn4(t, t - 1)

            between(act, step)
            attn1(T, T - 1)
            attn1b(T, T - 1)
            attn2(T, T - 1)
            attn3(T, T - 1)
            attn4(T, T - 1)

            def gelu(r, u):
                act.wait_ge(sem("hidden_ready"), UNROLL * r + u + 1)
                if not (isinstance(r, int) and r == 0 and u < 2):
                    act.wait_ge(sem("hidden_turned"), UNROLL * r + u - 1)
                nc.scalar.activation(hid[:, u % 2, :], pA[u % 2][:, :], ACT.Gelu).then_inc(sem("gelu_done"), 1)

            for u in range(UNROLL):
                gelu(0, u)
            with act.Fori(1, MOE_TILES // UNROLL) as r:
                for u in range(UNROLL):
                    gelu(r, u)
            for t in range(T):
                act.wait_ge(sem("sum_done"), t + 1)
                act.dma_start(out_d[:, t * P:(t + 1) * P, :].rearrange("b p c -> p b c"),
                              x_tok[:, :, t, :]).then_inc(sem("stored"), 16)
            act.wait_ge(sem("stored"), 16 * T)

        @block.tensor
        def _(pe):
            mm, tr = nc.tensor.matmul, nc.tensor.transpose
            pe.wait_ge(sem("ident_made"), 1)
            for i in range(8):
                bank, written = claim(pe, None, f"x{i}")
                pe.wait_ge(sem(f"x_loaded{i // 2}{i % 2}"), 16)
                for j in range(4):
                    last = tr(bank[:, P * j:P * j + P], x_tok[:, i // 2, 4 * (i % 2) + j, :], ident[:, :])
                last.then_inc(written, 1)
            bank, written = claim(pe, None, "wup")
            pe.wait_ge(sem("weights_loaded"), 16 * 28)
            for j in range(4):
                last = tr(bank[:, P * j:P * j + P], wup_n[:, j, :], ident[:, :])
            last.then_inc(written, 1)
            bank, written = claim(pe, None, "wdn")
            for j in range(2):
                last = tr(bank[:, P * j:P * j + P], wdn_n[:, P * j:P * j + P], ident[:, :])
            last.then_inc(written, 1)
            bank, written = claim(pe, None, "fcw")
            tr(bank[:, 0:C], fcw_n[:, :], ident[:, :]).then_inc(written, 1)
            pe.wait_ge(sem("bdT_made"), 6)
            for f in range(HALVES):
                bank, written = claim(pe, None, f"bd{f}")
                for w in range(3):
                    last = tr(bank[:, P * w:P * w + P], bdT[:, w, f, :], ident[:, :])
                last.then_inc(written, 1)
            bank, written = claim(pe, None, "gate")
            for j in range(6):
                last = tr(bank[:, 16 * j:16 * j + 16], wg_n[:, P * j:P * j + P], ident[0:16, 0:16])
            last.then_inc(written, 1)
            bank, written = claim(pe, None, "lnT")
            tr(bank[:, 0:2 * E], lngb_n[:, :], ident[0:16, 0:16]).then_inc(written, 1)
            bank, written = claim(pe, None, "gmean")
            pe.wait_ge(sem("gstats_done"), B)
            mm(bank[:, 0:B], avg4[:, :], gmv[:, :, 0], start=True, stop=True).then_inc(written, 1)
            bank, written = claim(pe, None, "gvar")
            pe.wait_ge(sem("gvar_in"), 1)
            mm(bank[:, 0:B], avg4[:, :], gv[:, :], start=True, stop=True).then_inc(written, 1)
            bank, written = claim(pe, None, "geffx")
            taken(pe, None, "gate")
            for f in range(HALVES):
                mm(bank[:, 16 * f:16 * f + 16], bdT[:, 0, f, :], wgT[:, f, :], start=True, stop=False)
                last = mm(bank[:, 16 * f:16 * f + 16], bdT[:, 1, f, :], wgT[:, 2 + f, :], start=False, stop=True)
            last.then_inc(written, 1)
            bank, written = claim(pe, None, "geffm")
            for f in range(HALVES):
                last = mm(bank[:, 16 * f:16 * f + 16], bdT[:, 2, f, :], wgT[:, 4 + f, :], start=True, stop=True)
            last.then_inc(written, 1)
            taken(pe, None, "lnT")
            pe.wait_ge(sem("w1_loaded"), 16)
            bank, written = claim(pe, None, "b1")
            for e in range(E):
                last = mm(bank[0:E, :], lnbdiag[:, E * e:E * e + E], w1[:, e, :], start=(e == 0), stop=(e == E - 1))
            last.then_inc(written, 1)

            def up(t, src, lo, names):
                for f in range(HALVES):
                    bank, written = claim(pe, src, names[f])
                    if isinstance(t, int):
                        rhs = xT[:, :, P * t:P * t + P]
                    else:
                        rhs = xT[:, :, bass.ds(t * P, P)]
                    mm(bank[:, :], wupT[:, lo + f, :], rhs, start=True, stop=True).then_inc(written, 1)

            def qkv(t, src):
                pe.wait_ge(sem("xact_ready"), 2 * t + 2)
                if src is None:
                    taken(pe, src, "xm1")
                for b in range(B):
                    bank, written = claim(pe, src, f"k{b}")
                    xmb = [xm[:, f, b, CONV - 1:] for f in range(HALVES)]
                    mm(bank[:, 0:P + 16], xact[:, 0, b, :], kg[:, 0, :], start=True, stop=False, skip_group_check=True)
                    mm(bank[:, P:INNER + 16], xact[:, 1, b, :], kg[:, 1, :], start=False, stop=False,
                       skip_group_check=True)
                    mm(bank[:, P:P + 16], xmb[0], mg[:, 0, :], start=False, stop=False, skip_group_check=True)
                    mm(bank[:, P:P + 16], xmb[1], mg[:, 1, :], start=False, stop=True,
                       skip_group_check=True).then_inc(written, 1)
                    bank, written = claim(pe, src, f"v{b}")
                    for f in range(HALVES):
                        last = mm(bank[:, P * f:P * f + P], xmb[f], bd[:, 2, f, :], start=True, stop=True)
                    last.then_inc(written, 1)

            def qkv2(t, src):
                bank, written = claim(pe, src, "gateT")
                for k in range(2):
                    last = tr(bank[0:BH, P * k:P * k + P], gates[:, k].rearrange("p b h -> p (b h)"), ident[:, :])
                last.then_inc(written, 1)
                for w, names in ((0, ("q0", "q1")), (1, ("kT0", "kT1"))):
                    for f in range(HALVES):
                        bank, written = claim(pe, src, names[f])
                        mm(bank[:, :], bd[:, w, f, :], xact[:, f].rearrange("p b i -> p (b i)"),
                           start=True, stop=True).then_inc(written, 1)

            def qkv3(t, src):
                for f in range(HALVES):
                    bank, written = claim(pe, src, f"uq{f}")
                    pe.wait_ge(sem("uq_ready"), t + 1)
                    for b in range(B):
                        last = mm(bank[:, P * b:P * b + P], spread[:, f, b].rearrange("p h d -> p (h d)"), uq[:, :], start=True, stop=True)
                    last.then_inc(written, 1)
                bank, written = claim(pe, src, "gtok")
                wait_apart(pe, sem("gm2_done"), 2 * t + 2)
                for k in range(2):
                    last = tr(bank[:, BH * k:BH * k + BH], gm2[:, k, :], ident[0:BH, 0:BH])
                last.then_inc(written, 1)

            def head(t, h):
                f, q = h // HPH, DH * (h % HPH)
                if not (isinstance(t, int) and t == 0 and h < 2):
                    pe.wait_ge(sem("decay_ready"), NH * t + h - 1)
                A = pA[h % 2]
                mm(A[:, :], parts[:, 0, :], bc(pick[:, h, :], 2, P), start=True, stop=False)
                mm(A[:, :], neghead[:, h:h + 1].broadcast_to([96, P]), cexp[:, :, :].rearrange("p b i -> p (b i)"), start=False, stop=False)
                mm(A[:, :], ident_b[:, :], maskneg[:, :, :].rearrange("p b i -> p (b i)"), start=False,
                   stop=True).then_inc(sem("exponents_ready"), 1)
                if not (isinstance(t, int) and t == 0 and h < 2):
                    pe.wait_ge(sem("weighted"), NH * t + h - 1)
                for b in range(B):
                    last = mm(pS[h % 2][:, P * b:P * b + P], kT[q:q + DH, f, b, :], qT[q:q + DH, f, b, :],
                              start=True, stop=True)
                last.then_inc(sem("scores_ready"), 1)

            def from_state(t, f):
                if not (isinstance(t, int) and t == 0 and f == 0):
                    pe.wait_ge(sem("half_copied"), 4 * t + 2 * f)
                for b in range(B):
                    mm(pO[b // 2][:, (b % 2) * HPH * DE:(b % 2 + 1) * HPH * DE], qpT[:, f, b, :],
                       KVm[:, f * B + b, :], start=(b % 2 == 0), stop=False, skip_group_check=True)

            def values(t, h):
                pe.wait_ge(sem("weighted"), NH * t + h + 1)
                for b in range(B):
                    o = (b % 2) * HPH * DE + (h % HPH) * DE
                    last = mm(pO[b // 2][:, o:o + DE], PT[:, h % 2, b, :], vext[:, b, h, :], start=False,
                              stop=(h % HPH == HPH - 1), skip_group_check=True)
                if h % HPH == HPH - 1:
                    last.then_inc(sem("half_ready"), 1)

            def state(t):
                pe.wait_ge(sem("vs_ready"), t + 1)
                for b in range(B):
                    bank = (pA + pS)[b]
                    for f in range(HALVES):
                        last = mm(bank[:, f * HPH * DE:(f + 1) * HPH * DE], ktok[:, b, P * f:P * f + P],
                                  vs[:, b, HPH * f:HPH * f + HPH, :].rearrange("p h d -> p (h d)"),
                                  start=True, stop=True)
                last.then_inc(sem("state_summed"), 1)

            def attn1(t, s):
                bank, written = claim(pe, t, "hnT")
                pe.wait_ge(sem("h1_ready"), B * s + B)
                for b in range(B):
                    last = tr(bank[:, P * b:P * b + P], hnm[:, b, :], ident[:, :])
                last.then_inc(written, 1)

            def attn1b(t, s):
                bank, written = claim(pe, t, "fc")
                taken(pe, t, "hnT")
                mm(bank[:, :], fcwT[:, :], hnmT[:, :, :].rearrange("p b i -> p (b i)"), start=True,
                   stop=True).then_inc(written, 1)

            def attn2(t, s):
                bank, written = claim(pe, t, "score")
                taken(pe, t, "fc")
                for b in range(B):
                    last = mm(bank[:, b:b + 1], qat[:, b, :], scw[:, :], start=True, stop=True)
                last.then_inc(written, 1)

            def attn3(t, s):
                bank, written = claim(pe, t, "tT")
                pe.wait_ge(sem("xt_ready"), B * s + B)
                for b in range(B):
                    last = tr(bank[:, P * b:P * b + P], xt[:, b, :], ident[:, :])
                last.then_inc(written, 1)

            def attn3b(t, s):
                bank, written = claim(pe, t, "logit")
                taken(pe, t, "tT")
                for b in range(B):
                    last = mm(bank[:, E * b:E * b + E], xtT[:, b, :], wr[:, :], start=True, stop=True)
                last.then_inc(written, 1)

            def attn4(t, s):
                bank, written = claim(pe, t, "count")
                pe.wait_ge(sem("sel_ready"), s + 1)
                mm(bank[:, 0:B * E], before[:, :], selb[:, :, :].rearrange("p b e -> p (b e)"), start=True,
                   stop=False, skip_group_check=True)
                for b in range(B):
                    for b2 in range(b + 1, B):
                        mm(bank[:, E * b2:E * b2 + E], ones_b[:, :], selb[:, b, :], start=False, stop=False,
                           skip_group_check=True)
                    last = mm(bank[:, B * E:B * E + E], ones_b[:, :], selb[:, b, :], start=False, stop=(b == B - 1),
                              skip_group_check=True)
                last.then_inc(written, 1)

            def turn_heads(t, s):
                for f in range(HALVES):
                    bank, written = claim(pe, t, f"y{f}")
                    pe.wait_ge(sem("hn_ready"), 2 * s + f + 1)
                    for b in range(B):
                        last = tr(bank[:, P * b:P * b + P],
                                  hn[:, b, HPH * f:HPH * f + HPH, :].rearrange("p h d -> p (h d)"), ident[:, :])
                    last.then_inc(written, 1)

            def down(t, s):
                for k in range(2):
                    bank, written = claim(pe, t, f"down{k}")
                    pe.wait_ge(sem("y_ready"), 2 * s + 2)
                    for b in range(2):
                        for f in range(HALVES):
                            last = mm(bank[:, P * b:P * b + P], yT[:, f, 2 * k + b, :], wdnT[:, f, :],
                                      start=(f == 0), stop=(f == 1))
                    last.then_inc(written, 1)

            pe.wait_ge(sem("xn_ready"), B)
            pe.wait_ge(sem("tables_made"), 1)
            pe.wait_ge(sem("pool_tables_made"), 1)
            up(0, None, 0, ("xm0", "xm1"))
            qkv(0, None)
            qkv2(0, None)
            qkv3(0, None)

            def step(t):
                first, last = (isinstance(t, int) and t == 0), (isinstance(t, int) and t == T - 1)
                pe.wait_ge(sem("parts_ready"), t + 1)
                if not first:
                    pe.wait_ge(sem("state_taken"), HALVES * B * t)
                head(t, 0)
                if not last:
                    up(t + 1, t, 0, ("xm0", "xm1"))
                head(t, 1)
                pe.wait_ge(sem("qp_ready"), 2 * t + 2)
                pe.wait_ge(sem("state_ready"), t + 1)
                from_state(t, 0)
                values(t, 0)
                head(t, 2)
                values(t, 1)
                if not first:
                    turn_heads(t, t - 1)
                head(t, 3)
                values(t, 2)
                if not first:
                    down(t, t - 1)
                values(t, 3)
                head(t, 4)
                head(t, 5)
                from_state(t, 1)
                values(t, 4)
                if not first:
                    attn1(t, t - 1)
                head(t, 6)
                values(t, 5)
                if not first:
                    attn1b(t, t - 1)
                head(t, 7)
                values(t, 6)
                if not first:
                    attn2(t, t - 1)
                up(t, t, 2, ("z0", "z1"))
                values(t, 7)
                pe.wait_ge(sem("decay_ready"), NH * t + NH)
                state(t)
                if not last:
                    qkv(t + 1, t)
                    qkv2(t + 1, t)
                if not first:
                    attn3(t, t - 1)
                    attn3b(t, t - 1)
                if not last:
                    qkv3(t + 1, t)
                if not first:
                    attn4(t, t - 1)

            between(pe, step)
            turn_heads(T, T - 1)
            down(T, T - 1)
            attn1(T, T - 1)
            attn1b(T, T - 1)
            attn2(T, T - 1)
            attn3(T, T - 1)
            attn3b(T, T - 1)
            attn4(T, T - 1)

            pe.wait_ge(sem("table_made"), 1)
            pe.wait_ge(sem("state_taken"), B * HALVES * T)
            pe.wait_ge(sem("w1_scaled"), E)
            pe.wait_ge(sem("w2_loaded"), 16 * E)
            pe.wait_ge(sem("bias3_made"), 48)

            def turn_in(r, u):
                pe.wait_ge(sem(f"rows_loaded{u}"), 16 * (r + 1))
                if not (isinstance(r, int) and r == 0 and u < 2):
                    pe.wait_ge(sem("xeT_ready"), 2 * UNROLL * r + u - 1)
                tr(pG[u % 2][:, 0:P], xin[:, u, 0:C], ident[:, :]).then_inc(sem("rows_turned"), 1)

            def hidden(r, u, e):
                i = 2 * UNROLL * r + u
                pe.wait_ge(sem("xeT_ready"), i + 1)
                if not (isinstance(r, int) and r == 0 and u < 2):
                    pe.wait_ge(sem("gelu_done"), i - 1)
                mm(pA[u % 2][:, :], xeT[:, u % 2, :], w1[:, bass.ds(e, 1), :].rearrange("p e f -> p (e f)"),
                   start=True, stop=False)
                mm(pA[u % 2][:, :], ones_b[0:3, :], bias3[:, bass.ds(e, 1), 0:F].rearrange("p e f -> p (e f)"),
                   start=False, stop=True).then_inc(sem("hidden_ready"), 1)

            def turn_hidden(r, u):
                i = 2 * UNROLL * r + u
                pe.wait_ge(sem("gelu_done"), i + 1)
                if not (isinstance(r, int) and r == 0 and u < 2):
                    pe.wait_ge(sem("hidT_ready"), i - 1)
                for k in range(FK):
                    last = tr(pS[u % 2][:, P * k:P * k + P], hid[:, u % 2, P * k:P * k + P], ident[:, :])
                last.then_inc(sem("hidden_turned"), 1)

            def result(r, u, e):
                i = 2 * UNROLL * r + u
                pe.wait_ge(sem("hidT_ready"), i + 1)
                if not (isinstance(r, int) and r == 0 and u < 2):
                    pe.wait_ge(sem("y_weighted"), i - 1)
                for k in range(FK):
                    mm(pO[u % 2][:, 0:C], hidT[:, u % 2, k, :],
                       w2[:, bass.ds(e, 1), k, :].rearrange("p e f -> p (e f)"), start=(k == 0), stop=False)
                mm(pO[u % 2][:, 0:C], ones_b[0:3, :], bias3[:, bass.ds(e, 1), F:F + C].rearrange("p e f -> p (e f)"),
                   start=False, stop=True).then_inc(sem("result_ready"), 1)

            def expert(i):
                return pe.value_load(table[0:1, 0, bass.ds(i, 1)], min_val=0, max_val=E - 1)

            U2 = 2 * UNROLL
            ROUNDS = MOE_TILES // U2

            def round_(r, more):
                for u in range(U2):
                    e = expert(r * U2 + u)
                    if u + 1 < U2:
                        turn_in(r, u + 1)
                    elif more:
                        turn_in(r + 1, 0)
                    hidden(r, u, e)
                    if u > 0:
                        result(r, u - 1, expert(r * U2 + u - 1))
                    elif not (isinstance(r, int) and r == 0):
                        result(r - 1, U2 - 1, expert(r * U2 - 1))
                    turn_hidden(r, u)

            turn_in(0, 0)
            round_(0, True)
            with pe.Fori(1, ROUNDS - 1) as r:
                round_(r, True)
            round_(ROUNDS - 1, False)
            result(ROUNDS - 1, U2 - 1, expert(MOE_TILES - 1))

        @block.vector
        def _(dve):
            v = nc.vector
            made = [0]

            def chain(ins):
                made[0] += 1
                ins.then_inc(sem("dve_chain"), 1)
                dve.wait_ge(sem("dve_chain"), made[0])

            chain(v.memset(lcar[:, :], 0.0))
            chain(v.memset(xm[:, :, :, :], 0.0))
            chain(v.memset(vext[:, :, :, :], 1.0))
            chain(v.memset(KV[:, :, :], 0.0))
            chain(v.memset(mhalf[:, :], -0.5))
            chain(v.memset(lnbdiag[:, :], 0.0))
            chain(v.memset(eones[:, :], 1.0))
            v.memset(KVm[:, :, :], 0.0).then_inc(sem("state_ready"), 1)
            for i in range(8):
                bank, n = use(None, f"x{i}")
                dve.wait_ge(sem(f"general{bank}_read"), n + 1)
                v.bn_stats(gst[:, i // 2, i % 2, :], xT[:, i // 2, 512 * (i % 2):512 * (i % 2) + 512]
                           ).then_inc(sem("gst_done"), 1)
            for b in range(B):
                dve.wait_ge(sem("gst_done"), 2 * b + 2)
                v.bn_aggr(gmv[:, b, :], gst[:, b, :, :].rearrange("p k s -> p (k s)")).then_inc(sem("gstats_done"), 1)
            dve.wait_ge(sem("weights_loaded"), 16 * 28)
            dve.wait_ge(sem("block4_made"), 1)
            for w in range(3):
                for f in range(HALVES):
                    v.tensor_tensor(bdT[:, w, f, :].rearrange("p (n d) -> p n d", d=4),
                                    block4[:, :].rearrange("p (n d) -> p n d", d=4),
                                    bc(wqkv_n[:, w, f, :], 1, 32), ALU.mult).then_inc(sem("bdT_made"), 1)
            for f in range(HALVES):
                bank, read = arrived(dve, None, f"bd{f}")
                v.tensor_copy(bd[:, :, f, :], bank[:, 0:3 * P].rearrange("p (w c) -> p w c", w=3)).then_inc(read, 1)
            bank, read = arrived(dve, None, "gate")
            v.tensor_copy(wgT[:, :, :].rearrange("p j g -> p (j g)"), bank[:, 0:96]).then_inc(read, 1)
            bank, read = arrived(dve, None, "lnT")
            chain(v.tensor_copy(lnbdiag[:, 0:E * E:E + 1], bank[:, E:2 * E]))
            v.tensor_copy(lngbT[:, :], bank[:, 0:2 * E]).then_inc(read, 1)
            bank, read = arrived(dve, None, "gmean")
            v.tensor_copy(gm[:, :], bank[:, 0:B]).then_inc(read, 1)
            taken(dve, None, "gmean")
            chain(v.tensor_tensor(gd[:, :], gmv[:, :, 0], gm[:, :], ALU.subtract))
            chain(v.tensor_tensor(gd[:, :], gd[:, :], gd[:, :], ALU.mult))
            v.tensor_tensor(gv[:, :], gd[:, :], gmv[:, :, 1], ALU.add).then_inc(sem("gvar_in"), 1)
            bank, read = arrived(dve, None, "gvar")
            v.tensor_scalar(gr[:, :], bank[:, 0:B], GN_EPS, None, ALU.add).then_inc(read, 1)
            dve.wait_ge(sem("gr_done"), 1)
            for b in range(B):
                v.tensor_scalar(xT[:, b, :], xT[:, b, :], gm[:, b:b + 1], gr[:, b:b + 1], ALU.subtract, ALU.mult
                                ).then_inc(sem("xn_ready"), 1)
            bank, read = arrived(dve, None, "geffx")
            chain(v.tensor_copy(kg[:, 0, P:P + 16], bank[:, 0:16]))
            v.tensor_copy(kg[:, 1, 0:16], bank[:, 16:32]).then_inc(read, 1)
            bank, read = arrived(dve, None, "geffm")
            v.tensor_copy(mg[:, :, :].rearrange("p f g -> p (f g)"), bank[:, 0:32]).then_inc(read, 1)
            taken(dve, None, "geffm")
            taken(dve, None, "bd0")
            taken(dve, None, "bd1")
            chain(v.tensor_copy(kg[:, 0, 0:P], bd[:, 1, 0, :]))
            v.tensor_copy(kg[:, 1, 16:P + 16], bd[:, 1, 1, :]).then_inc(sem("tables_made"), 1)
            bank, read = arrived(dve, None, "b1")
            v.tensor_tensor(bias[:, 0:F], bias[:, 0:F], bank[0:E, :], ALU.add).then_inc(read, 1)
            taken(dve, None, "b1")
            for k in range(3):
                chain(v.tensor_copy(bparts[:, k, :], bias[:, :]))
                if k < 2:
                    chain(v.tensor_tensor(bias[:, :], bias[:, :], bparts[:, k, :], ALU.subtract))
            v.memset(wks[:, :], 1.0).then_inc(sem("bparts_made"), 1)
            for e in range(E):
                v.tensor_scalar(w1[:, e, :], w1[:, e, :], lngbT[:, e:e + 1], None, ALU.mult
                                ).then_inc(sem("w1_scaled"), 1)

            def halo(t):
                for f in range(HALVES):
                    if isinstance(t, int) and t == 0:
                        v.memset(xm[:, f, :, 0:CONV - 1], 0.0).then_inc(sem("halo_moved"), 1)
                    else:
                        v.tensor_copy(xm[:, f, :, 0:CONV - 1], xm[:, f, :, P:P + CONV - 1]).then_inc(sem("halo_moved"), 1)

            def conv(t, src, halves=range(HALVES)):
                for f in halves:
                    taken(dve, src, f"xm{f}")
                    v.tensor_scalar(cacc[:, f], xm[:, f, :, 0:P], convw[:, f, 0:1], vecs[:, 0, f:f + 1],
                                    ALU.mult, ALU.add).then_inc(sem("tap_done"), 1)
                    for k in range(1, CONV):
                        dve.wait_ge(sem("tap_done"), 2 * (CONV - 1) * t + (CONV - 1) * f + k)
                        v.scalar_tensor_tensor(cacc[:, f], xm[:, f, :, k:k + P], convw[:, f, k:k + 1], cacc[:, f],
                                               ALU.mult, ALU.add
                                               ).then_inc(sem("tap_done" if k < CONV - 1 else "conv_done"), 1)

            def gate(t, src):
                taken(dve, src, "gateT")
                if isinstance(t, int) and t == 0:
                    v.memset(rcar[:, 0:1], NEG).then_inc(sem("gate_chain"), 1)
                else:
                    v.tensor_copy(rcar[:, 0:1], gc[:, 1, P - 1:P]).then_inc(sem("gate_chain"), 1)
                v.tensor_scalar(fmin[:, :], gpre[:, 1, :], 0.0, None, ALU.min
                                ).then_inc(sem("gate_chain"), 1)
                dve.wait_ge(sem("fln_done"), t + 1)
                dve.wait_ge(sem("gate_chain"), 10 * t + 2)
                v.tensor_tensor_scan(lc[:, :], fmin[:, :], fabs[:, :], lcar[:, 0:1], ALU.add, ALU.subtract
                                     ).then_inc(sem("gate_chain"), 1)
                dve.wait_ge(sem("gate_chain"), 10 * t + 3)
                v.tensor_copy(lcar[:, :], lc[:, P - 1:P]).then_inc(sem("gate_chain"), 1)
                v.tensor_tensor(gc[:, 0, :], gpre[:, 0, :], lc[:, :], ALU.subtract).then_inc(sem("g_done"), 1)
                dve.wait_ge(sem("g_done"), t + 1)
                dve.wait_ge(sem("gate_chain"), 10 * t + 4)
                v.tensor_tensor_scan(gc[:, 1, :], gc[:, 0, :], gc[:, 0, :], rcar[:, 0:1], ALU.max, ALU.max
                                     ).then_inc(sem("c_ready"), 1)
                dve.wait_ge(sem("c_ready"), t + 1)
                v.tensor_scalar(rcar[:, 1:2], gc[:, 1, P - 1:P], -1.0, None, ALU.mult).then_inc(sem("r_end_ready"), 1)
                v.tensor_tensor(fmin[:, :], lc[:, :], gc[:, 1, :], ALU.add).then_inc(sem("m_ready"), 1)
                v.tensor_copy(parts[0:BH], gc[:, :, :]).then_inc(sem("gate_chain"), 1)
                dve.wait_ge(sem("gate_chain"), 10 * t + 5)
                v.tensor_tensor(r1[:, :, :], gc[:, :, :], parts[0:BH], ALU.subtract).then_inc(sem("gate_chain"), 1)
                dve.wait_ge(sem("gate_chain"), 10 * t + 6)
                v.tensor_copy(parts[BH:2 * BH], r1[:, :, :]).then_inc(sem("gate_chain"), 1)
                v.tensor_copy(gmid[:, :, :], r1[:, :, :]).then_inc(sem("gate_chain"), 1)
                dve.wait_ge(sem("gate_chain"), 10 * t + 8)
                v.tensor_tensor(r2[:, :, :], r1[:, :, :], gmid[:, :, :], ALU.subtract).then_inc(sem("gate_chain"), 1)
                dve.wait_ge(sem("gate_chain"), 10 * t + 9)
                v.tensor_copy(parts[2 * BH:3 * BH], r2[:, :, :]).then_inc(sem("gate_chain"), 1)
                dve.wait_ge(sem("gate_chain"), 10 * t + 10)
                v.tensor_tensor(cexp[:, :, :], bc(parts[:, 1, :], 1, B), bc(ofbatch[:, :], 2, P), ALU.mult
                                ).then_inc(sem("parts_ready"), 1)

            def qprime(t, src):
                for f in range(HALVES):
                    bank, read = arrived(dve, src, f"uq{f}")
                    taken(dve, src, f"q{f}")
                    v.tensor_tensor(qpT[:, f].rearrange("p b i -> p (b i)"), qT[:, f].rearrange("p b i -> p (b i)"),
                                    bank[:, :], ALU.mult).then_inc(sem("qp_ready"), 1)
                    v.tensor_copy(decay[:, f, :], bank[:, :].rearrange("p (b i) -> p b i", b=B)[:, :, P - 1]
                                  ).then_inc(read, 1)

            def weigh(t, h):
                dve.wait_ge(sem("decay_ready"), NH * t + h + 1)
                dve.wait_ge(sem("scores_ready"), NH * t + h + 1)
                v.tensor_tensor(PT[:, h % 2].rearrange("p b i -> p (b i)"), pS[h % 2][:, :],
                                D[:, h % 2].rearrange("p b i -> p (b i)"), ALU.mult).then_inc(sem("weighted"), 1)

            def new_state(t):
                dve.wait_ge(sem("state_summed"), t + 1)
                for b in range(B):
                    for f in range(HALVES):
                        v.scalar_tensor_tensor(KV[:, f * B + b, :], KV[:, f * B + b, :], decay[:, f, b:b + 1],
                                               (pA + pS)[b][:, f * HPH * DE:(f + 1) * HPH * DE],
                                               ALU.mult, ALU.add).then_inc(sem("state_taken"), 1)

            def norm_a(t, f):
                o, num = osb[:, f], osb[:, f, :, :, 0:DH]
                dve.wait_ge(sem("half_copied"), 4 * t + 2 * f + 2)
                expm = gtok[:, 1, :, HPH * f:HPH * f + HPH]
                v.scalar_tensor_tensor(nrm[:, f], o[:, :, :, DH], -1.0, expm, ALU.mult, ALU.max
                                       ).then_inc(sem("norm_taken"), 1)
                v.tensor_reduce(mu[:, f], num, AX.X, ALU.add).then_inc(sem("norm_chain"), 1)
                dve.wait_ge(sem("norm_taken"), 2 * t + f + 1)
                v.tensor_tensor(nrm[:, f], nrm[:, f], o[:, :, :, DH], ALU.max).then_inc(sem("norm_chain"), 1)
                dve.wait_ge(sem("norm_chain"), 8 * (2 * t + f) + 2)
                v.tensor_scalar(nrm[:, f], nrm[:, f], ROW_EPS, None, ALU.add).then_inc(sem("norm_chain"), 1)
                v.tensor_scalar(mu[:, f], mu[:, f], 1.0 / DH, None, ALU.mult).then_inc(sem("norm_chain"), 1)
                dve.wait_ge(sem("norm_chain"), 8 * (2 * t + f) + 3)
                v.reciprocal(rr[:, f], nrm[:, f]).then_inc(sem("norm_chain"), 1)
                dve.wait_ge(sem("norm_chain"), 8 * (2 * t + f) + 4)
                v.tensor_tensor(dd[:, f].rearrange("p b h d -> p (b h) d"), num.rearrange("p b h d -> p (b h) d"),
                                bc(mu[:, f].rearrange("p b h -> p (b h)"), 2, DH), ALU.subtract
                                ).then_inc(sem("norm_read"), 1)

            def norm_b(t, f):
                dve.wait_ge(sem("dsq_done"), 2 * t + f + 1)
                v.tensor_reduce(var[:, f], dsq[:, f], AX.X, ALU.add).then_inc(sem("norm_chain"), 1)
                dve.wait_ge(sem("norm_chain"), 8 * (2 * t + f) + 6)
                v.tensor_tensor(var[:, f], var[:, f], rr[:, f], ALU.mult).then_inc(sem("norm_chain"), 1)
                dve.wait_ge(sem("norm_chain"), 8 * (2 * t + f) + 7)
                v.tensor_tensor(var[:, f], var[:, f], rr[:, f], ALU.mult).then_inc(sem("norm_chain"), 1)
                dve.wait_ge(sem("norm_chain"), 8 * (2 * t + f) + 8)
                v.tensor_scalar(var[:, f], var[:, f], 1.0 / DH, LN_EPS, ALU.mult, ALU.add).then_inc(sem("var_c"), 1)

            def norm2(t, f):
                dve.wait_ge(sem("rstd_ready"), 2 * t + f + 1)
                v.tensor_tensor(rr[:, f], rr[:, f], var[:, f], ALU.mult).then_inc(sem("scale_done"), 1)
                dve.wait_ge(sem("scale_done"), 2 * t + f + 1)
                v.tensor_tensor(hn[:, :, HPH * f:HPH * f + HPH, :], dd[:, f], bc(rr[:, f], 3, DH), ALU.mult
                                ).then_inc(sem("hn_ready"), 1)

            def gated(t, s, f):
                bank, read = arrived(dve, t, f"y{f}")
                dve.wait_ge(sem("sx_ready"), s + 1)
                y = yT[:, f].rearrange("p b i -> p (b i)")
                v.scalar_tensor_tensor(y, bank[:, :], vecs[:, 1, f:f + 1], sx[:, f].rearrange("p b i -> p (b i)"),
                                       ALU.mult, ALU.add).then_inc(read, 1)
                taken(dve, t, f"y{f}")
                v.tensor_tensor(y, y, sz[:, f].rearrange("p b i -> p (b i)"), ALU.mult).then_inc(sem("y_ready"), 1)

            def row(t, b):
                if isinstance(t, int):
                    return x_tok[:, b, t, :]
                return x_tok[:, b, bass.ds(t, 1), :].rearrange("p a c -> p (a c)")

            def xtok(t, k):
                if isinstance(t, int):
                    return x_tok[:, 2 * k:2 * k + 2, t, :]
                return x_tok[:, 2 * k:2 * k + 2, bass.ds(t, 1), :].rearrange("p b a c -> p b (a c)")

            def residual(t, s):
                for k in range(2):
                    bank, read = arrived(dve, t, f"down{k}")
                    v.tensor_tensor(x1[:, 2 * k:2 * k + 2, :], xtok(s, k), bank[:, 0:2 * C].rearrange(
                        "p (b c) -> p b c", b=2), ALU.add).then_inc(read, 1)
                taken(dve, t, "down0")
                taken(dve, t, "down1")
                for b in range(B):
                    v.bn_stats(st1[:, b, :], x1[:, b, :]).then_inc(sem("residual_chain"), 1)
                for b in range(B):
                    wait_apart(dve, sem("residual_chain"), 2 * B * s + b + 1)
                    v.bn_aggr(mv1[:, b, :], st1[:, b, :]).then_inc(sem("residual_chain"), 1)
                dve.wait_ge(sem("residual_chain"), 2 * B * s + 2 * B)
                v.tensor_scalar(rs1[:, :], mv1[:, :, 1], LN_EPS, None, ALU.add).then_inc(sem("var1_ready"), 1)

            def attn1(t, s):
                dve.wait_ge(sem("rs1_ready"), s + 1)
                for b in range(B):
                    v.tensor_scalar(hnm[:, b, :], x1[:, b, :], mv1[:, b, 0:1], rs1[:, b:b + 1], ALU.subtract,
                                    ALU.mult).then_inc(sem("h1_ready"), 1)

            def attn2(t, s):
                bank, read = arrived(dve, t, "score")
                v.tensor_copy(esc[:, :], bank[:, 0:B]).then_inc(read, 1)
                taken(dve, t, "score")
                v.tensor_tensor_scan(emax[:, :], esc[:, :], esc[:, :], NEG, ALU.max, ALU.max
                                     ).then_inc(sem("softmax_chain"), 1)
                dve.wait_ge(sem("softmax_chain"), 6 * s + 1)
                v.tensor_tensor(wat[:, :, :], bc(esc[:, :], 1, B), bc(emax[:, :], 2, B), ALU.subtract
                                ).then_inc(sem("softmax_chain"), 1)
                dve.wait_ge(sem("softmax_chain"), 6 * s + 2)
                v.tensor_scalar(wat[:, :, :], wat[:, :, :], 0.0, None, ALU.min).then_inc(sem("wat_ready"), 1)

            def attn3(t, s):
                dve.wait_ge(sem("wat_exp"), s + 1)
                v.tensor_tensor(wat[:, :, :], wat[:, :, :], causal4[:, :, :], ALU.mult).then_inc(sem("softmax_chain"), 1)
                dve.wait_ge(sem("softmax_chain"), 6 * s + 3)
                v.tensor_reduce(wsum[:, :], wat[:, :, :], AX.X, ALU.add).then_inc(sem("softmax_chain"), 1)
                dve.wait_ge(sem("softmax_chain"), 6 * s + 4)
                v.reciprocal(wsum[:, :], wsum[:, :]).then_inc(sem("softmax_chain"), 1)
                dve.wait_ge(sem("softmax_chain"), 6 * s + 5)
                v.tensor_tensor(wat[:, :, :], wat[:, :, :], bc(wsum[:, :], 2, B), ALU.mult).then_inc(sem("softmax_chain"), 1)
                dve.wait_ge(sem("softmax_chain"), 6 * s + 6)
                for k in range(B):
                    for b in range(k, B):
                        if k > 0:
                            dve.wait_ge(sem("mixed"), 10 * s + sum(B - j for j in range(k - 1)) + (b - k + 1) + 1)
                        v.scalar_tensor_tensor(row(s, b), hnm[:, k, :], wat[:, b, k:k + 1],
                                               x1[:, b, :] if k == 0 else row(s, b), ALU.mult, ALU.add
                                               ).then_inc(sem("mixed"), 1)
                wait_apart(dve, sem("mixed"), 10 * s + 10)
                for b in range(B):
                    v.bn_stats(st3[:, b, :], row(s, b)).then_inc(sem("stats3_chain"), 1)
                for b in range(B):
                    wait_apart(dve, sem("stats3_chain"), 2 * B * s + b + 1)
                    v.bn_aggr(mv3[:, b, :], st3[:, b, :]).then_inc(sem("stats3_chain"), 1)
                dve.wait_ge(sem("stats3_chain"), 2 * B * s + 2 * B)
                v.tensor_scalar(rs3[:, :], mv3[:, :, 1], LN_EPS, None, ALU.add).then_inc(sem("var3_ready"), 1)

            def attn4(t, s):
                dve.wait_ge(sem("rs3_ready"), s + 1)
                for b in range(B):
                    v.tensor_scalar(xt[:, b, :], row(s, b), mv3[:, b, 0:1], rs3[:, b:b + 1], ALU.subtract,
                                    ALU.mult).then_inc(sem("xt_ready"), 1)
                v.tensor_tensor(v2[:, :], rs3[:, :], rs3[:, :], ALU.mult).then_inc(sem("variance_chain"), 1)
                dve.wait_ge(sem("variance_chain"), 2 * s + 1)
                v.tensor_tensor(v2[:, :], v2[:, :], mv3[:, :, 1], ALU.mult).then_inc(sem("variance_chain"), 1)
                dve.wait_ge(sem("variance_chain"), 2 * s + 2)
                v.tensor_scalar(v2[:, :], v2[:, :], LN_EPS, None, ALU.add).then_inc(sem("v2_ready"), 1)

            def attn5(t, s):
                bank, read = arrived(dve, t, "logit")
                v.tensor_tensor(lg[:, :, :], bank[:, 0:B * E].rearrange("p (b e) -> p b e", b=B), bc(brb[:, :], 1, B),
                                ALU.add).then_inc(read, 1)
                taken(dve, t, "logit")
                v.tensor_reduce(lmax[:, :], lg[:, :, :], AX.X, ALU.max).then_inc(sem("rank_chain"), 1)
                other = bc(lg[:, :, :], 2, E)
                own = bc(lg[:, :, :], 3, E)
                v.tensor_tensor(cmp[:, :, :, :], other, own, ALU.is_gt).then_inc(sem("rank_chain"), 1)
                v.tensor_tensor(ceq[:, :, :, :], other, own, ALU.is_equal).then_inc(sem("rank_chain"), 1)
                dve.wait_ge(sem("rank_chain"), 6 * s + 1)
                v.tensor_tensor(pex[:, :, :], lg[:, :, :], bc(lmax[:, :], 2, E), ALU.subtract
                                ).then_inc(sem("pex_ready"), 1)
                dve.wait_ge(sem("rank_chain"), 6 * s + 3)
                v.tensor_tensor(ceq[:, :, :, :].rearrange("p b e f -> p b (e f)"),
                                ceq[:, :, :, :].rearrange("p b e f -> p b (e f)"),
                                bc(lower8[:, :, :].rearrange("p e f -> p (e f)"), 1, B), ALU.mult
                                ).then_inc(sem("rank_chain"), 1)
                dve.wait_ge(sem("rank_chain"), 6 * s + 4)
                v.tensor_tensor(cmp[:, :, :, :], cmp[:, :, :, :], ceq[:, :, :, :], ALU.add).then_inc(sem("rank_chain"), 1)
                dve.wait_ge(sem("rank_chain"), 6 * s + 5)
                v.tensor_reduce(rank[:, :, :], cmp[:, :, :, :], AX.X, ALU.add).then_inc(sem("rank_chain"), 1)
                dve.wait_ge(sem("rank_chain"), 6 * s + 6)
                for k in range(2):
                    v.tensor_scalar(oh[:, k], rank[:, :, :], float(k), None, ALU.is_equal).then_inc(sem("oh_done"), 1)
                v.tensor_scalar(selb[:, :, :], rank[:, :, :], 1.5, None, ALU.is_lt).then_inc(sem("sel_ready"), 1)

            def attn6(t, s):
                bank, read = arrived(dve, t, "count")
                v.tensor_tensor(pos[:, :, :], bank[:, 0:B * E].rearrange("p (b e) -> p b e", b=B),
                                bc(offs[:, :], 1, B), ALU.add).then_inc(sem("route_chain"), 1)
                dve.wait_ge(sem("route_chain"), 7 * s + 1)
                v.tensor_tensor(offs[:, :], offs[:, :], bank[:, B * E:B * E + E], ALU.add).then_inc(read, 1)
                dve.wait_ge(sem("pex_exp"), s + 1)
                dve.wait_ge(sem("oh_done"), 2 * s + 2)
                v.tensor_tensor(tmpk[:, :, :, :].rearrange("p k b e -> p k (b e)"),
                                oh[:, :, :, :].rearrange("p k b e -> p k (b e)"),
                                bc(pex[:, :, :].rearrange("p b e -> p (b e)"), 1, 2), ALU.mult
                                ).then_inc(sem("route_chain"), 1)
                dve.wait_ge(sem("route_chain"), 7 * s + 2)
                v.tensor_reduce(wk[:, :, :], tmpk[:, :, :, :], AX.X, ALU.add).then_inc(sem("route_chain"), 1)
                dve.wait_ge(sem("route_chain"), 7 * s + 3)
                v.tensor_tensor(wks[:, :], wk[:, 0, :], wk[:, 1, :], ALU.add).then_inc(sem("route_chain"), 1)
                dve.wait_ge(sem("route_chain"), 7 * s + 4)
                v.reciprocal(wks[:, :], wks[:, :]).then_inc(sem("route_chain"), 1)
                if not (isinstance(s, int) and s == 0):
                    for k in range(2):
                        for b in range(B):
                            dve.wait_ge(sem(f"scattered{k}{b}"), 16 * s)
                dve.wait_ge(sem("route_chain"), 7 * s + 5)
                v.tensor_tensor(xrow[:, :, :, C].rearrange("p b k -> p k b"), wk[:, :, :], bc(wks[:, :], 1, 2),
                                ALU.mult).then_inc(sem("row_part"), 1)
                v.tensor_copy(xrow[:, :, :, C + 1].bitcast(I32), dest[:, :, :]).then_inc(sem("row_part"), 1)
                dve.wait_ge(sem("row_part"), (2 + B) * s + 2)
                v.tensor_scalar(dest[:, :, :], dest[:, :, :], float(P), None, ALU.add)
                dve.wait_ge(sem("rs4_ready"), s + 1)
                for b in range(B):
                    v.tensor_scalar(xrow[:, b, :, 0:C], bc(xt[:, b, :], 1, 2), rs4[:, b:b + 1], None, ALU.mult
                                    ).then_inc(sem("row_part"), 1)
                v.tensor_tensor(tmpk[:, :, :, :].rearrange("p k b e -> p k (b e)"),
                                oh[:, :, :, :].rearrange("p k b e -> p k (b e)"),
                                bc(pos[:, :, :].rearrange("p b e -> p (b e)"), 1, 2), ALU.mult
                                ).then_inc(sem("route_chain"), 1)
                dve.wait_ge(sem("route_chain"), 7 * s + 6)
                v.tensor_reduce(slotf[:, :, :], tmpk[:, :, :, :], AX.X, ALU.add).then_inc(sem("route_chain"), 1)
                dve.wait_ge(sem("route_chain"), 7 * s + 7)
                v.tensor_copy(slot[:, :, :], slotf[:, :, :]).then_inc(sem("slots_ready"), 1)

            dve.wait_ge(sem("pool_tables_made"), 1)
            dve.wait_ge(sem("bias3_made"), 48)
            halo(0)
            conv(0, None)
            gate(0, None)
            qprime(0, None)
            chain(v.tensor_copy(offs[:, :], region0[:, :]))

            def step(t):
                first, last = (isinstance(t, int) and t == 0), (isinstance(t, int) and t == T - 1)
                if not last:
                    halo(t + 1)
                weigh(t, 0)
                if not first:
                    norm2(t - 1, 0)
                    norm2(t - 1, 1)
                weigh(t, 1)
                if not last:
                    conv(t + 1, t, [0])
                weigh(t, 2)
                if not first:
                    gated(t, t - 1, 0)
                    gated(t, t - 1, 1)
                weigh(t, 3)
                if not last:
                    conv(t + 1, t, [1])
                if not first:
                    residual(t, t - 1)
                weigh(t, 4)
                weigh(t, 5)
                if not first:
                    attn1(t, t - 1)
                weigh(t, 6)
                norm_a(t, 0)
                weigh(t, 7)
                if not first:
                    attn2(t, t - 1)
                norm_b(t, 0)
                new_state(t)
                norm_a(t, 1)
                if not first:
                    attn3(t, t - 1)
                    attn4(t, t - 1)
                if not last:
                    gate(t + 1, t)
                if not first:
                    attn5(t, t - 1)
                if not last:
                    qprime(t + 1, t)
                norm_b(t, 1)
                if not first:
                    attn6(t, t - 1)

            between(dve, step)
            for f in range(HALVES):
                norm2(T - 1, f)
            for f in range(HALVES):
                gated(T, T - 1, f)
            residual(T, T - 1)
            attn1(T, T - 1)
            attn2(T, T - 1)
            attn3(T, T - 1)
            attn4(T, T - 1)
            attn5(T, T - 1)
            attn6(T, T - 1)

            taken(dve, T, "count")
            chain(v.tensor_copy(tailrow[:, :], offs[0:1, :]))
            v.tensor_tensor(cnt[:, :], offs[0:1, :], region0[0:1, :], ALU.subtract).then_inc(sem("tails_known"), 1)
            dve.wait_ge(sem("tails_known"), 1)
            chain(v.tensor_scalar(tls[:, :], cnt[:, :], 1.0 / P, (P - 1.0) / P - 0.5 + 0.5 / P, ALU.mult, ALU.add))
            chain(v.tensor_copy(tlsi[:, :], tls[:, :]))
            chain(v.tensor_copy(tls[:, :], tlsi[:, :]))
            chain(v.tensor_tensor_scan(tend[:, :], eones[:, :], tls[:, :], 0.0, ALU.mult, ALU.add))
            chain(v.tensor_tensor(tbeg[:, :], tend[:, :], tls[:, :], ALU.subtract))
            tile_i = bc(til[:, :], 2, E)
            chain(v.tensor_tensor(past[:, :, :], bc(tend[:, :], 1, MOE_TILES), tile_i, ALU.is_le))
            chain(v.tensor_reduce(tef[:, :], past[:, :, :], AX.X, ALU.add))
            chain(v.tensor_scalar(table[:, 0, :], tef[:, :], float(E - 1), None, ALU.min))
            chain(v.tensor_tensor(ina[:, :, :], bc(tbeg[:, :], 1, MOE_TILES), tile_i, ALU.is_le))
            chain(v.tensor_tensor(ina[:, :, :], ina[:, :, :], past[:, :, :], ALU.subtract))
            chain(v.tensor_tensor(rowt[:, :, :], tile_i, bc(tbeg[:, :], 1, MOE_TILES), ALU.subtract))
            chain(v.tensor_scalar(rowt[:, :, :], rowt[:, :, :], float(P), None, ALU.mult))
            chain(v.tensor_tensor(rowt[:, :, :], rowt[:, :, :], bc(region0[0:1, :], 1, MOE_TILES), ALU.add))
            chain(v.tensor_tensor(rowt[:, :, :], rowt[:, :, :], ina[:, :, :], ALU.mult))
            chain(v.tensor_reduce(trf[:, :], rowt[:, :, :], AX.X, ALU.add))
            chain(v.tensor_scalar(tef[:, :], tef[:, :], E - 0.5, float(E * REGION), ALU.is_gt, ALU.mult))
            v.tensor_tensor(table[:, 1, :], trf[:, :], tef[:, :], ALU.add).then_inc(sem("table_made"), 1)

            U2 = 2 * UNROLL

            def rows_in(r, u):
                i = U2 * r + u
                dve.wait_ge(sem("rows_turned"), i + 1)
                if not (isinstance(r, int) and r == 0 and u < 2):
                    dve.wait_ge(sem("hidden_ready"), i - 1)
                v.tensor_copy(xeT[:, u % 2, :], pG[u % 2][:, 0:P]).then_inc(sem("xeT_ready"), 1)

            def hid_in(r, u):
                i = U2 * r + u
                dve.wait_ge(sem("hidden_turned"), i + 1)
                if not (isinstance(r, int) and r == 0 and u < 2):
                    dve.wait_ge(sem("result_ready"), i - 1)
                v.tensor_copy(hidT[:, u % 2].rearrange("p k i -> p (k i)"), pS[u % 2][:, :]
                              ).then_inc(sem("hidT_ready"), 1)

            def y_out(r, u):
                i = U2 * r + u
                dve.wait_ge(sem("result_ready"), i + 1)
                if not (isinstance(r, int) and r == 0 and u < UNROLL):
                    dve.wait_ge(sem(f"y_sent{(u - UNROLL) % U2}"), 16 * (r + (0 if u < UNROLL else 1)))
                v.tensor_scalar(yout[:, u % UNROLL, :], pO[u % 2][:, 0:C], xin[:, u, C:C + 1], None, ALU.mult
                                ).then_inc(sem("y_weighted"), 1)

            def round_(r, more):
                for u in range(U2):
                    if u + 1 < U2:
                        rows_in(r, u + 1)
                    elif more:
                        rows_in(r + 1, 0)
                    hid_in(r, u)
                    if u > 0:
                        y_out(r, u - 1)
                    elif not (isinstance(r, int) and r == 0):
                        y_out(r - 1, U2 - 1)

            ROUNDS = MOE_TILES // U2
            rows_in(0, 0)
            round_(0, True)
            with dve.Fori(1, ROUNDS - 1) as r:
                round_(r, True)
            round_(ROUNDS - 1, False)
            y_out(ROUNDS - 1, U2 - 1)

            for t in range(T):
                dve.wait_ge(sem(f"y_loaded{t % 4}"), 32 * (t // 4 + 1))
                v.tensor_tensor(x_tok[:, :, t, :], x_tok[:, :, t, :], ya[:, t % 4, 0], ALU.add
                                ).then_inc(sem("sum_a"), 1)
                dve.wait_ge(sem("sum_a"), t + 1)
                v.tensor_tensor(x_tok[:, :, t, :], x_tok[:, :, t, :], ya[:, t % 4, 1], ALU.add
                                ).then_inc(sem("sum_done"), 1)

        @block.gpsimd
        def _(pool):
            g = nc.gpsimd
            made = [0]

            def chain(ins):
                made[0] += 1
                ins.then_inc(sem("pool_chain"), 1)
                pool.wait_ge(sem("pool_chain"), made[0])

            def select(ap, pattern, op, fill, base, cm):
                return g.affine_select(ap, ap, pattern, op, fill, base, cm)

            chain(g.memset(ident[:, :], 0.0))
            select(ident[:, :], [[1, P]], ALU.not_equal, 1.0, 0, -1).then_inc(sem("ident_made"), 1)
            chain(g.memset(block4[:, :], 1.0))
            chain(select(block4[:, :], [[-4, 32], [0, 4]], ALU.is_ge, 0.0, 0, 1))
            chain(select(block4[:, :], [[4, 32], [0, 4]], ALU.is_ge, 0.0, 3, -1))
            g.tensor_scalar(avg4[:, :], block4[:, :], 0.25, 0.0, ALU.mult, ALU.add).then_inc(sem("block4_made"), 1)
            pool.wait_ge(sem("ident_made"), 1)
            chain(g.tensor_copy(ident_b[:, :], ident[:, :]))
            chain(g.memset(maskneg[:, :, :], 0.0))
            chain(select(maskneg[:, :, :], [[0, B], [1, P]], ALU.is_ge, NEG, 0, -1))
            chain(g.memset(ones_b[:, :], 1.0))
            chain(g.memset(before[:, :], 1.0))
            chain(select(before[:, :], [[1, P]], ALU.is_ge, 0.0, -1, -1))
            taken(pool, None, "gvar")
            g.tensor_tensor(gr[:, :], gr[:, :], mhalf[:, 0:B], ALU.pow).then_inc(sem("gr_done"), 1)
            chain(g.memset(headmask[:, :, :], 1.0))
            hm = headmask[:, :, :]
            chain(select(hm, [[-DH, HPH], [0, DE]], ALU.is_ge, 0.0, 0, 1))
            chain(select(hm, [[DH, HPH], [0, DE]], ALU.is_ge, 0.0, DH - 1, -1))
            chain(g.memset(pick[:, :, :], 0.0))
            for k in range(3):
                chain(select(pick[BH * k:BH * k + BH, :, :], [[1, NH], [NH, B]], ALU.not_equal, 1.0, 0, -1))
            chain(g.memset(spread[:, :, :, :, :], 0.0))
            for f in range(HALVES):
                chain(select(spread[:, f], [[NH, B], [1, HPH], [0, DH]], ALU.not_equal, 1.0, HPH * f, -1))
            chain(g.tensor_tensor(hsum[:, :], pick[:, :, 0], pick[:, :, 1], ALU.add))
            chain(g.tensor_tensor(hsum[:, :], hsum[:, :], pick[:, :, 2], ALU.add))
            chain(g.tensor_tensor(hsum[:, :], hsum[:, :], pick[:, :, 3], ALU.add))
            chain(g.tensor_scalar(neghead[:, :], hsum[:, :], -1.0, 0.0, ALU.mult, ALU.add))
            chain(g.tensor_tensor(ofbatch[:, :], pick[:, 0, :], pick[:, 1, :], ALU.add))
            for h in range(2, NH):
                chain(g.tensor_tensor(ofbatch[:, :], ofbatch[:, :], pick[:, h, :], ALU.add))
            chain(g.memset(lower8[:, :, :], 1.0))
            chain(select(lower8[:, :, :], [[1, E], [-1, E]], ALU.is_ge, 0.0, -1, 0))
            chain(g.memset(causal4[:, :, :], 1.0))
            chain(select(causal4[:, :, :], [[1, B], [-1, B]], ALU.is_ge, 0.0, 0, 0))
            chain(g.iota(iota8[:, :], [[REGION, E]], 0, 0))
            chain(g.tensor_copy(region0[:, :], iota8[:, :]))
            chain(g.iota(iota8[:, :], [[S, B], [TOK, 2]], 0, 1))
            chain(g.tensor_copy(dest[:, :, :].rearrange("p b k -> p (b k)"), iota8[:, :]))
            chain(g.iota(iotat[:, :], [[1, MOE_TILES]], 0, 0))
            chain(g.tensor_copy(til[:, :], iotat[:, :]))
            chain(g.memset(tail[:, :], 0.0))
            chain(g.iota(tail[:, C + 1:C + 2].bitcast(I32), [[0, 1]], SKIP, 0))
            g.memset(tail[:, C:C + 1], 0.0).then_inc(sem("pool_tables_made"), 1)

            def values_scaled(t):
                w = gtok[:, 0].rearrange("p b h -> p (b h)")
                g.tensor_tensor(vs[:, :, :, :].rearrange("p b h d -> p (b h) d"),
                                vext[:, :, :, :].rearrange("p b h d -> p (b h) d"), bc(w, 2, DE), ALU.mult
                                ).then_inc(sem("vs_ready"), 1)

            def square(t, f):
                pool.wait_ge(sem("norm_read"), 2 * t + f + 1)
                g.tensor_tensor(dsq[:, f].rearrange("p b h d -> p (b h d)"), dd[:, f].rearrange("p b h d -> p (b h d)"),
                                dd[:, f].rearrange("p b h d -> p (b h d)"), ALU.mult).then_inc(sem("dsq_done"), 1)

            def rsqrt(ap, n, ready, count, done):
                pool.wait_ge(sem(ready), count)
                g.tensor_tensor(ap, ap, mhalf[:, 0:n], ALU.pow).then_inc(sem(done), 1)

            def scatter(s):
                wait_apart(pool, sem("slots_ready"), s + 1)
                wait_apart(pool, sem("row_part"), (2 + B) * (s + 1))
                for k in range(2):
                    for b in range(B):
                        g.indirect_dma_start(
                            xs, bass.IndirectOffsetOnAxis(slot[:, k, b:b + 1].bitcast(U32), 0), xrow[:, b, k, :], None
                        ).then_inc(sem(f"scattered{k}{b}"), 16)

            def late(s):
                rsqrt(rs3[:, :], B, "var3_ready", s + 1, "rs3_ready")

            def late2(s):
                pool.wait_ge(sem("v2_ready"), s + 1)
                g.tensor_tensor(rs4[:, :], v2[:, :], mhalf[:, 0:B], ALU.pow).then_inc(sem("rs4_ready"), 1)

            def head_rstd(t, f):
                rsqrt(var[:, f].rearrange("p b h -> p (b h)"), B * HPH, "var_c", 2 * t + f + 1, "rstd_ready")

            def row_rstd(s):
                rsqrt(rs1[:, :], B, "var1_ready", s + 1, "rs1_ready")

            def step(t):
                first = isinstance(t, int) and t == 0
                pool.wait_ge(sem("gscale_ready"), t + 1)
                values_scaled(t)
                wait_apart(pool, sem("xact_ready"), 2 * t + 2)
                if not first:
                    wait_apart(pool, sem("y_ready"), 2 * t)
                for f in range(HALVES):
                    g.tensor_scalar(sx[:, f], xact[:, f], vecs[:, 2, f:f + 1], 0.0, ALU.mult, ALU.add
                                    ).then_inc(sem("sx_ready" if f else "sx_half"), 1)
                if not first:
                    row_rstd(t - 1)
                square(t, 0)
                head_rstd(t, 0)
                pool.wait_ge(sem("state_taken"), B * HALVES * (t + 1))
                g.tensor_tensor(KVm[:, :, :], KV[:, :, :],
                                bc(headmask[:, :, :].rearrange("p h d -> p (h d)"), 1, HALVES * B),
                                ALU.mult).then_inc(sem("state_ready"), 1)
                square(t, 1)
                if not first:
                    late(t - 1)
                    late2(t - 1)
                head_rstd(t, 1)
                if not first:
                    scatter(t - 1)

            between(pool, step)
            row_rstd(T - 1)
            late(T - 1)
            late2(T - 1)
            scatter(T - 1)

            def send(r, u):
                wait_apart(pool, sem("y_weighted"), 2 * UNROLL * r + u + 1)
                g.indirect_dma_start(
                    y2, bass.IndirectOffsetOnAxis(xin[:, u, C + 1:C + 2].bitcast(U32), 0), yout[:, u % UNROLL, :],
                    None, bounds_check=2 * TOK - 1, oob_is_err=False).then_inc(sem(f"y_sent{u}"), 16)

            for u in range(2 * UNROLL):
                send(0, u)
            with pool.Fori(1, MOE_TILES // (2 * UNROLL)) as r:
                for u in range(2 * UNROLL):
                    send(r, u)


_INS = ['x', 'L0_conv_W_up', 'L0_conv_conv_w', 'L0_conv_conv_b', 'L0_conv_Wq', 'L0_conv_Wk', 'L0_conv_Wv',
        'L0_conv_W_i', 'L0_conv_b_i', 'L0_conv_W_f', 'L0_conv_b_f', 'L0_conv_norm_w', 'L0_conv_skip',
        'L0_conv_W_down', 'L1_attn_fc_w', 'L1_attn_fc_b', 'L1_attn_score_w', 'L1_ffn_Wr', 'L1_ffn_br',
        'L1_ffn_ln_g', 'L1_ffn_ln_b', 'L1_ffn_W1', 'L1_ffn_b1', 'L1_ffn_W2', 'L1_ffn_b2']


def kernel(**inputs):
    import numpy as _np
    import concourse.bacc as _bacc
    from concourse import mybir as _mybir
    from concourse.bass_utils import run_bass_kernel_spmd as _run

    nc = _bacc.Bacc("TRN2", target_bir_lowering=False, num_devices=1)
    arrays, args = {}, {}
    for name in _INS:
        arr = _np.ascontiguousarray(inputs[name])
        arrays[f"in_{name}"] = arr
        args[name] = nc.dram_tensor(f"in_{name}", arr.shape, _mybir.dt.from_np(arr.dtype), kind="ExternalInput").ap()
    out = nc.dram_tensor("out_0", (B, 32, 32, C), _mybir.dt.float32, kind="ExternalOutput").ap()
    block_kernel(nc, args, out)
    r = _run(nc, [arrays], core_ids=[0])
    return r.results[0]["out_0"]
```

```python
from contextlib import ExitStack

import concourse.bass as bass
from concourse import mybir

ALU = mybir.AluOpType
ACT = mybir.ActivationFunctionType
AX = mybir.AxisListType
F32 = mybir.dt.float32
BF16 = mybir.dt.bfloat16
I32 = mybir.dt.int32
U32 = mybir.dt.uint32

P = 128
B = 4
C = 128
S = 1024
T = S // P
N = B * P
TOK = B * S
INNER = 256
HALVES = INNER // P
NH = 8
DH = INNER // NH
HPH = NH // HALVES
DE = DH + 1
BH = B * NH
CONV = 4
E = 8
F = 512
FK = F // P
SUBS = 1
ROWS = SUBS * P
REGION = TOK + ROWS
XW = C + 2
MOE_TILES = 2 * TOK // ROWS + E
UNROLL = 8
OUTS = 4
WBUFS = 4
EBITS = 3
ROUNDS = MOE_TILES // UNROLL
SKIP = 1 << 20
NEG = -1.0e30
GN_EPS = 1e-5
LN_EPS = 1e-5
ROW_EPS = 1e-6


def bc(ap, axis, n):
    shape = list(ap.shape)
    shape.insert(axis, n)
    return ap.unsqueeze(axis).broadcast_to(shape)


class Ring:

    NEXT_X = ["xm0", "xm1"]
    NEXT_K = ["k0", "v0", "k1", "v1", "k2", "v2", "k3", "v3", "gateT", "q0", "q1", "kT0", "kT1"]
    NEXT_U = ["uq0", "uq1", "gtok"]
    ORDER = ([(n, "next") for n in NEXT_X]
             + [(n, "late") for n in ("y0", "y1", "down0", "down1", "hnT", "fc", "score")]
             + [("z0", "now"), ("z1", "now")] + [(n, "next") for n in NEXT_K]
             + [("tT", "late"), ("logit", "late")] + [(n, "next") for n in NEXT_U] + [("count", "late")])

    def __init__(self, prologue):
        self.names = {"first": self.pick("now", "next"), "middle": self.pick("now", "next", "late"),
                      "last": self.pick("now", "late"), "end": self.pick("late")}
        self.names["last"].remove("count")
        self.names["end"].insert(self.names["end"].index("fc") + 1, "count_before")
        self.per = len(self.names["middle"])
        self.base = {"first": prologue, "middle": prologue + len(self.names["first"])}
        self.base["last"] = self.base["middle"] + (T - 2) * self.per
        self.base["end"] = self.base["last"] + len(self.names["last"])
        assert prologue % 2 == 0 and len(self.names["first"]) % 2 == 0 and self.per % 2 == 0

    def pick(self, *stages):
        return [n for n, stage in self.ORDER if stage in stages]

    def use(self, t, name):
        kind = {0: "first", T - 1: "last", T: "end"}.get(t, "middle") if isinstance(t, int) else "middle"
        n = self.base[kind] + self.names[kind].index(name)
        return n % 2, (n // 2 + (t - 1) * (self.per // 2) if kind == "middle" else n // 2)


def block_kernel(nc, a, out):
    ctx = ExitStack()
    with ctx:
        def sb(name, shape, dt=F32):
            return ctx.enter_context(nc.sbuf_tensor(name, shape, dt))

        def pb(name, shape, dt=F32):
            return ctx.enter_context(nc.psum_tensor(name, shape, dt))

        sems = {}

        def sem(name):
            if name not in sems:
                sems[name] = ctx.enter_context(nc.semaphore(name))
            return sems[name]

        xs = nc.dram_tensor("expert_rows", [E * REGION + ROWS, XW], F32).ap()
        y2 = nc.dram_tensor("expert_out", [2 * TOK, C], F32).ap()
        x_d = a["x"].rearrange("b h w c -> b (h w) c")
        out_d = out.rearrange("b h w c -> b (h w) c")

        ident = sb("ident", [P, P])
        ident_b = sb("ident_b", [P, P], BF16)
        block4 = sb("block4", [P, P])
        avg4 = sb("avg4", [P, P])
        maskneg = sb("maskneg", [P, B, P], BF16)
        before = sb("before", [P, P], BF16)
        ones_b = sb("ones_b", [P, P], BF16)
        headmask = sb("headmask", [P, HPH, DE])
        pick = sb("pick", [96, NH, B], BF16)
        neghead = sb("neghead", [96, NH], BF16)
        ofbatch = sb("ofbatch", [96, B], BF16)
        spread = sb("spread", [BH, HALVES, B, HPH, DH])
        lower8 = sb("lower8", [P, E, E])
        mhalf = sb("mhalf", [P, N // P * 8])
        causal4 = sb("causal4", [P, B, B])
        region0 = sb("region0", [P, E])
        dest = sb("dest", [P, B, 2])
        tail = sb("tail", [P, XW])
        hsum = sb("hsum", [96, NH], BF16)
        iota8 = sb("iota8", [P, 8], I32)
        iotat = sb("iotat", [1, MOE_TILES], I32)

        wupT = sb("wupT", [C, 4, P])
        wdnT = sb("wdnT", [P, HALVES, C])
        fcwT = sb("fcwT", [C, C])
        wqkv_n = sb("wqkv_n", [P, 3, HALVES, 4])
        bd = sb("bd", [P, 3, HALVES, P])
        wgT = sb("wgT", [P, 6, 2 * NH])
        kg = sb("kg", [P, HALVES, P + 2 * NH])
        mg = sb("mg", [P, HALVES, 2 * NH])
        vecs = sb("vecs", [P, 3, HALVES])
        convw = sb("convw", [P, HALVES, CONV])
        fcb = sb("fcb", [C, 1])
        scw = sb("scw", [C, 1])
        bif = sb("bif", [BH, 2])
        wr = sb("wr", [C, E])
        brb = sb("brb", [P, E])
        lngbT = sb("lngbT", [C, 2 * E])
        w1 = sb("w1", [C, E, F])
        w2 = sb("w2", [P, E, FK, C])
        b1T = sb("b1T", [P, FK, E])
        b2n = sb("b2n", [E, C])
        b2p = sb("b2p", [3, E, C], BF16)
        b1f = sb("b1f", [P, WBUFS, FK])
        b2f = sb("b2f", [3, WBUFS, C], BF16)

        x_tok = sb("x_tok", [P, B, T, C])
        xT = sb("xT", [C, B, S])
        gst = sb("gst", [C, B, 2, 6])
        gmv = sb("gmv", [C, B, 2])
        gm = sb("gm", [C, B])
        gd = sb("gd", [C, B])
        gv = sb("gv", [C, B])
        gr = sb("gr", [C, B])
        xm = sb("xm", [P, HALVES, B, CONV - 1 + P])
        cacc = sb("cacc", [P, HALVES, B, P])
        xact = sb("xact", [P, HALVES, B, P])
        sx = sb("sx", [P, HALVES, B, P])
        sz = sb("sz", [P, HALVES, B, P])
        qT = sb("qT", [P, HALVES, B, P])
        qpT = sb("qpT", [P, HALVES, B, P])
        kT = sb("kT", [P, HALVES, B, P])
        ktok = sb("ktok", [P, B, INNER])
        vext = sb("vext", [P, B, NH, DE])
        vs = sb("vs", [P, B, NH, DE])
        gates = sb("gates", [P, 2, B, NH])
        fabs = sb("fabs", [BH, P])
        fmin = sb("fmin", [BH, P])
        gpre = sb("gpre", [BH, 2, P])
        lcar = sb("lcar", [BH, 1])
        lc = sb("lc", [BH, P])
        gc = sb("gc", [BH, 2, P])
        rcar = sb("rcar", [BH, 2])
        r1 = sb("r1", [BH, 2, P])
        r2 = sb("r2", [BH, 2, P])
        gmid = sb("gmid", [BH, 2, P], BF16)
        parts = sb("parts", [96, 2, P], BF16)
        cexp = sb("cexp", [96, B, P], BF16)
        uq = sb("uq", [BH, P])
        gm2 = sb("gm2", [BH, 2, P])
        gtok = sb("gtok", [P, 2, B, NH])
        decay = sb("decay", [P, HALVES, B])
        D = sb("D", [P, 2, B, P])
        PT = sb("PT", [P, 2, B, P])
        KV = sb("KV", [P, HALVES * B, HPH * DE])
        KVm = sb("KVm", [P, HALVES * B, HPH * DE])
        osb = sb("osb", [P, 2, B, HPH, DE])
        nrm = sb("nrm", [P, 2, B, HPH])
        rr = sb("rr", [P, 2, B, HPH])
        mu = sb("mu", [P, 2, B, HPH])
        dd = sb("dd", [P, 2, B, HPH, DH])
        dsq = sb("dsq", [P, 2, B, HPH, DH])
        var = sb("var", [P, 2, B, HPH])
        hn = sb("hn", [P, B, NH, DH])
        yT = sb("yT", [P, HALVES, B, P])
        x1 = sb("x1", [P, B, C])
        st1 = sb("st1", [P, B, 6])
        mv1 = sb("mv1", [P, B, 2])
        rs1 = sb("rs1", [P, B])
        hnm = sb("hnm", [P, B, C])
        hnmT = sb("hnmT", [C, B, P])
        qat = sb("qat", [C, B, P])
        esc = sb("esc", [P, B])
        emax = sb("emax", [P, B])
        wat = sb("wat", [P, B, B])
        wsum = sb("wsum", [P, B])
        st3 = sb("st3", [P, B, 6])
        mv3 = sb("mv3", [P, B, 2])
        rs3 = sb("rs3", [P, B])
        v2 = sb("v2", [P, B])
        rs4 = sb("rs4", [P, B])
        xt = sb("xt", [P, B, C])
        xtT = sb("xtT", [C, B, P])
        lg = sb("lg", [P, B, E])
        lmax = sb("lmax", [P, B])
        cmp = sb("cmp", [P, B, E, E])
        ceq = sb("ceq", [P, B, E, E])
        rank = sb("rank", [P, B, E])
        oh = sb("oh", [P, 2, B, E])
        selb = sb("selb", [P, B, E], BF16)
        pex = sb("pex", [P, B, E])
        wk = sb("wk", [P, 2, B])
        wks = sb("wks", [P, B])
        tmpk = sb("tmpk", [P, 2, B, E])
        pos = sb("pos", [P, B, E])
        offs = sb("offs", [P, E])
        slotf = sb("slotf", [P, 2, B])
        slot = sb("slot", [P, 2, B], I32)
        xrow = sb("xrow", [P, B, 2, XW])

        cnt = sb("cnt", [1, E])
        tls = sb("tls", [1, E])
        tlsi = sb("tlsi", [1, E], I32)
        tend = sb("tend", [1, E])
        tbeg = sb("tbeg", [1, E])
        eones = sb("eones", [1, E])
        til = sb("til", [1, MOE_TILES])
        tef = sb("tef", [1, MOE_TILES])
        trf = sb("trf", [1, MOE_TILES])
        firstrow = sb("firstrow", [1, MOE_TILES], I32)
        tex = sb("tex", [1, MOE_TILES + 2])
        texi = sb("texi", [1, 2], I32)
        power = sb("power", [1, UNROLL])
        digits = sb("digits", [1, ROUNDS, UNROLL])
        aheadf = sb("aheadf", [1, ROUNDS])
        ahead = sb("ahead", [1, ROUNDS], I32)
        tailrow = sb("tailrow", [1, E], I32)

        def over(buf, lo, *shape):
            flat = buf[:] if len(buf.shape) == 2 else buf[:].rearrange(
                {3: "p a b -> p (a b)", 4: "p a b c -> p (a b c)", 5: "p a b c d -> p (a b c d)"}[len(buf.shape)])
            n = 1
            for d in shape[1:]:
                n *= d
            v = flat[0:shape[0], lo:lo + n]
            if len(shape) == 3:
                return v.rearrange("p (a b) -> p a b", a=shape[1])
            if len(shape) == 4:
                return v.rearrange("p (a b c) -> p a b c", a=shape[1], b=shape[2])
            return v

        wup_n = over(hn, 0, P, 4, C)
        wdn_n = over(hn, 4 * C, C, INNER)
        fcw_n = over(hn, 4 * C + INNER, C, C)
        bdT = over(dd, 0, P, 3, HALVES, P)
        wg_n = over(dsq, 0, 2 * NH, 3 * INNER)
        lngb_n = over(dsq, 3 * INNER, 2 * E, C)
        b1n = over(xrow, 0, E, F)
        bparts = over(xrow.bitcast(BF16), 2 * F, E, 3, C)
        past = over(qT, 0, 1, MOE_TILES, E)
        ina = over(kT, 0, 1, MOE_TILES, E)
        rowt = over(cacc, 0, 1, MOE_TILES, E)
        xin = [over(vs, 0, P, 4, SUBS, XW), over(vext, 0, P, 4, SUBS, XW)]
        hidT = [over(sz, 0, P, FK, ROWS), over(sx, 0, P, FK, ROWS)]
        yout = over(yT, 0, P, OUTS, SUBS, C)
        xeT = over(osb, 0, C, WBUFS, ROWS)
        w1f = [over(buf, F * i, C, F) for buf in (D, xact) for i in range(2)]
        w2f = [over(buf, F * i, P, FK * C) for buf in (PT, qpT) for i in range(2)]
        ya = [over(xT, 2 * B * C * i, P, 2 * B * C) for i in range(4)]
        ya += [over(buf, 0, P, 2 * B * C) for buf in (kT, qT, hn, ktok)]
        ya = [buf.rearrange("p (g c) -> p g c", c=C) for buf in ya]

        pG = [pb(f"pG{i}", [P, 512]) for i in range(2)]
        pA = [pb(f"pA{i}", [P, 512]) for i in range(2)]
        pS = [pb(f"pS{i}", [P, 512]) for i in range(2)]
        pO = [pb(f"pO{i}", [P, 512]) for i in range(2)]

        PRO = ([f"x{i}" for i in range(8)] + ["wup", "wdn", "fcw", "bd0", "bd1", "gate", "lnT"]
               + ["gmean", "gvar", "geffx", "geffm"] + ["b1"]
               + Ring.NEXT_X + Ring.NEXT_K + Ring.NEXT_U)
        ring = Ring(len(PRO))

        def use(t, name):
            if t is None:
                n = PRO.index(name)
                return n % 2, n // 2
            return ring.use(t, name)

        def claim(eng, t, name):
            bank, n = use(t, name)
            if not (isinstance(n, int) and n == 0):
                eng.wait_ge(sem(f"general{bank}_read"), n)
            return pG[bank], sem(f"general{bank}_written")

        def arrived(eng, t, name):
            bank, n = use(t, name)
            eng.wait_ge(sem(f"general{bank}_written"), n + 1)
            return pG[bank], sem(f"general{bank}_read")

        def taken(eng, t, name):
            bank, n = use(t, name)
            eng.wait_ge(sem(f"general{bank}_read"), n + 1)

        def wait_apart(eng, semaphore, value):
            eng.wait_ge(semaphore, value)
            if not isinstance(value, int):
                eng.sem_inc(sem("waits_apart"), 1)

        def g(src, pat=None, **kw):
            return a[src].rearrange(pat, **kw) if pat else a[src]

        block = ctx.enter_context(nc.Block())

        def between(eng, step):
            step(0)
            with eng.Fori(1, T - 1) as t:
                step(t)
            step(T - 1)

        @block.sync
        def _(sp):
            for b in range(B):
                for h in range(2):
                    sp.dma_start(x_tok[:, b, 4 * h:4 * h + 4, :],
                                 x_d[b, 512 * h:512 * h + 512, :].rearrange("(t p) c -> p t c", p=P)
                                 ).then_inc(sem(f"x_loaded{b}{h}"), 16)
            with nc.allow_non_contiguous_dma(reason="small weights, once"):
                for dst, src in [
                    (vecs[:, 0], g("L0_conv_conv_b", "(f p) -> p f", p=P)),
                    (vecs[:, 1], g("L0_conv_norm_w", "(f p) -> p f", p=P)),
                    (vecs[:, 2], g("L0_conv_skip", "(f p) -> p f", p=P)),
                    (convw[:, :, :], g("L0_conv_conv_w", "(f p) a k -> p f (a k)", p=P)),
                    (fcb[:, :], g("L1_attn_fc_b", "(p a) -> p a", a=1)),
                    (scw[:, :], g("L1_attn_score_w", "(p a) -> p a", a=1)),
                    (wr[:, :], g("L1_ffn_Wr")),
                    (brb[:, :], g("L1_ffn_br", "(a e) -> a e", a=1).broadcast_to([P, E])),
                    (lngb_n[0:E, :], g("L1_ffn_ln_g")),
                    (lngb_n[E:2 * E, :], g("L1_ffn_ln_b")),
                    (b1n[:, :], g("L1_ffn_b1")),
                    (b2n[:, :], g("L1_ffn_b2")),
                ] + [(bif[NH * b:NH * b + NH, k:k + 1], g(("L0_conv_b_i", "L0_conv_b_f")[k], "(h a) -> h a", a=1))
                     for b in range(B) for k in range(2)]:
                    sp.dma_start(dst, src).then_inc(sem("vectors_loaded"), 16)
            sp.dma_start(w1[:, :, :], a["L1_ffn_W1"].rearrange("e d f -> d e f")).then_inc(sem("w1_loaded"), 16)
            for e in range(E):
                sp.dma_start(w2[:, e, :, :], a["L1_ffn_W2"][e].rearrange("(k p) d -> p k d", p=P)
                             ).then_inc(sem("w2_loaded"), 16)

            sp.wait_ge(sem("bparts_made"), 1)
            for k in range(3):
                sp.dma_start(b2p[k:k + 1, :, :], bparts[:, k:k + 1, :]).then_inc(sem("b2p_made"), 16)

            sp.wait_ge(sem("tails_known"), 1)
            sp.wait_ge(sem("pool_tables_made"), 1)
            for e in range(E):
                row = sp.value_load(tailrow[0:1, e:e + 1], min_val=0, max_val=E * REGION - ROWS)
                sp.dma_start(xs[bass.ds(row, ROWS), :].rearrange("(j p) c -> p j c", p=P), bc(tail[:, :], 1, SUBS)
                             ).then_inc(sem("tails_written"), 16)
            sp.dma_start(xs[E * REGION:E * REGION + ROWS, :].rearrange("(j p) c -> p j c", p=P),
                         bc(tail[:, :], 1, SUBS)).then_inc(sem("tails_written"), 16)
            sp.wait_ge(sem("tails_written"), 16 * (E + 1))
            for k in range(2):
                for b in range(B):
                    sp.wait_ge(sem(f"scattered{k}{b}"), 16 * T)
            sp.wait_ge(sem("table_made"), 1)

            def load(i, u):
                row = sp.value_load(firstrow[0:1, bass.ds(i, 1)], min_val=0, max_val=E * REGION)
                sp.dma_start(xin[u // 4][:, u % 4], xs[bass.ds(row, ROWS), :].rearrange("(j p) c -> p j c", p=P)
                             ).then_inc(sem(f"rows_loaded{u}"), 16)

            for u in range(UNROLL):
                load(u, u)
            with sp.Fori(1, ROUNDS) as r:
                for u in range(UNROLL):
                    sp.wait_ge(sem(f"y_sent{u}"), 16 * SUBS * r)
                    load(r * UNROLL + u, u)

            for u in range(UNROLL):
                sp.wait_ge(sem(f"y_sent{u}"), 16 * SUBS * ROUNDS)
            for t in range(T):
                sp.dma_start(ya[t], y2.rearrange("(kb t p) c -> t p kb c", kb=2 * B, p=P)[t]
                             ).then_inc(sem(f"y_loaded{t}"), 16)

        @block.scalar
        def _(act):
            with nc.allow_non_contiguous_dma(reason="small weights, once"):
                for dst, src in [
                    (wup_n[:, :, :], g("L0_conv_W_up", "(o p) c -> p o c", p=P)),
                    (wdn_n[:, :], g("L0_conv_W_down")),
                    (fcw_n[:, :], g("L1_attn_fc_w")),
                    (wqkv_n[:, 0], g("L0_conv_Wq", "(f n) o d -> (n o) f d", f=HALVES)),
                    (wqkv_n[:, 1], g("L0_conv_Wk", "(f n) o d -> (n o) f d", f=HALVES)),
                    (wqkv_n[:, 2], g("L0_conv_Wv", "(f n) o d -> (n o) f d", f=HALVES)),
                    (wg_n[0:NH, :], g("L0_conv_W_i")),
                    (wg_n[NH:2 * NH, :], g("L0_conv_W_f")),
                ]:
                    act.dma_start(dst, src).then_inc(sem("matrices_loaded"), 16)

            for i in range(8):
                bank, read = arrived(act, None, f"x{i}")
                nc.scalar.activation(xT[:, i // 2, 512 * (i % 2):512 * (i % 2) + 512], bank[:, :],
                                     ACT.Copy).then_inc(read, 1)
            bank, read = arrived(act, None, "wup")
            nc.scalar.activation(wupT[:, :, :].rearrange("p o c -> p (o c)"), bank[:, :], ACT.Copy).then_inc(read, 1)
            bank, read = arrived(act, None, "wdn")
            nc.scalar.activation(wdnT[:, :, :].rearrange("p o c -> p (o c)"), bank[:, 0:256],
                                 ACT.Copy).then_inc(read, 1)
            bank, read = arrived(act, None, "fcw")
            nc.scalar.activation(fcwT[:, :], bank[:, 0:C], ACT.Copy).then_inc(read, 1)

            def first_tap(t, src):
                for f in range(HALVES):
                    taken(act, src, f"xm{f}")
                    nc.scalar.activation(cacc[:, f], xm[:, f, :, 0:P], ACT.Identity, bias=vecs[:, 0, f:f + 1],
                                         scale=convw[:, f, 0:1]).then_inc(sem("tap0_done"), 1)

            def silu_x(t):
                for f in range(HALVES):
                    act.wait_ge(sem("conv_done"), 2 * t + f + 1)
                    nc.scalar.activation(xact[:, f], cacc[:, f], ACT.Silu).then_inc(sem("xact_ready"), 1)

            def xm_copy(t, src):
                for f in range(HALVES):
                    bank, read = arrived(act, src, f"xm{f}")
                    act.wait_ge(sem("halo_moved"), 2 * t + f + 1)
                    nc.scalar.activation(xm[:, f, :, CONV - 1:], bank[:, :].rearrange("p (b i) -> p b i", b=B),
                                         ACT.Copy).then_inc(read, 1)

            def qkv(t, src):
                for b in range(B):
                    bank, read = arrived(act, src, f"k{b}")
                    if b == 0 and not (isinstance(t, int) and t == 0):
                        act.wait_ge(sem("state_summed"), t)
                    nc.scalar.activation(ktok[:, b, :].rearrange("p (f c) -> p f c", f=2),
                                         bank[:, 0:2 * (P + 16)].rearrange("p (f c) -> p f c", f=2)[:, :, 0:P],
                                         ACT.Copy).then_inc(sem("ktok_part"), 1)
                    nc.scalar.activation(gates[:, :, b, :],
                                         bank[:, P:P + 16].rearrange("p (k h) -> p k h", k=2),
                                         ACT.Copy).then_inc(read, 1)
                    bank, read = arrived(act, src, f"v{b}")
                    nc.scalar.activation(vext[:, b, :, 0:DH], bank[:, 0:INNER].rearrange("p (h d) -> p h d", h=NH),
                                         ACT.Copy).then_inc(read, 1)

            def qkv2(t, src):
                bank, read = arrived(act, src, "gateT")
                nc.scalar.activation(fabs[:, :], bank[0:BH, P:2 * P], ACT.Abs, bias=bif[:, 1:2]
                                     ).then_inc(sem("fabs_done"), 1)
                for k in range(2):
                    ins = nc.scalar.activation(gpre[:, k, :], bank[0:BH, P * k:P * k + P], ACT.Identity,
                                               bias=bif[:, k:k + 1])
                    ins.then_inc(*((sem("gpre_i_ready"), 1) if k == 0 else (read, 1)))
                act.wait_ge(sem("fabs_done"), t + 1)
                nc.scalar.activation(fabs[:, :], fabs[:, :], ACT.Exp, scale=-1.0).then_inc(sem("fexp_done"), 1)
                act.wait_ge(sem("fexp_done"), t + 1)
                nc.scalar.activation(fabs[:, :], fabs[:, :], ACT.Ln, bias=1.0).then_inc(sem("fln_done"), 1)
                for n, (name, dst) in enumerate([("q0", qT[:, 0]), ("q1", qT[:, 1]),
                                                 ("kT0", kT[:, 0]), ("kT1", kT[:, 1])]):
                    bank, read = arrived(act, src, name)
                    nc.scalar.activation(dst.rearrange("p b i -> p (b i)"), bank[:, :], ACT.Copy,
                                         scale=DH ** -0.5 if n < 2 else 1.0).then_inc(read, 1)

            def qkv3(t, src):
                act.wait_ge(sem("c_ready"), t + 1)
                nc.scalar.activation(uq[:, :], gc[:, 1, :], ACT.Exp, bias=rcar[:, 0:1], scale=-1.0
                                     ).then_inc(sem("uq_ready"), 1)
                act.wait_ge(sem("r_end_ready"), t + 1)
                nc.scalar.activation(gm2[:, 0, :], gc[:, 0, :], ACT.Exp, bias=rcar[:, 1:2]
                                     ).then_inc(sem("gm2_done"), 1)
                act.wait_ge(sem("m_ready"), t + 1)
                nc.scalar.activation(gm2[:, 1, :], fmin[:, :], ACT.Exp, scale=-1.0).then_inc(sem("gm2_done"), 1)
                bank, read = arrived(act, src, "gtok")
                if not (isinstance(t, int) and t == 0):
                    act.wait_ge(sem("norm_taken"), 2 * t)
                nc.scalar.activation(gtok[:, 0].rearrange("p b h -> p (b h)"), bank[:, 0:BH],
                                     ACT.Copy).then_inc(sem("gscale_ready"), 1)
                nc.scalar.activation(gtok[:, 1].rearrange("p b h -> p (b h)"), bank[:, BH:2 * BH],
                                     ACT.Copy).then_inc(read, 1)

            def exps(t, h):
                act.wait_ge(sem("exponents_ready"), NH * t + h + 1)
                if not (isinstance(t, int) and t == 0 and h < 2):
                    act.wait_ge(sem("weighted"), NH * t + h - 1)
                nc.scalar.activation(D[:, h % 2].rearrange("p b i -> p (b i)"), pA[h % 2][:, :], ACT.Exp
                                     ).then_inc(sem("decay_ready"), 1)

            def out_copy(t, f):
                act.wait_ge(sem("half_ready"), 2 * t + f + 1)
                if not (isinstance(t, int) and t == 0):
                    act.wait_ge(sem("norm_read"), 2 * t + f - 1)
                for k in range(2):
                    nc.scalar.activation(osb[:, f, 2 * k:2 * k + 2].rearrange("p b h d -> p (b h d)"),
                                         pO[k][:, 0:2 * HPH * DE], ACT.Copy).then_inc(sem("half_copied"), 1)

            def attn1(t, s):
                bank, read = arrived(act, t, "hnT")
                nc.scalar.activation(hnmT[:, :, :].rearrange("p b i -> p (b i)"), bank[:, :], ACT.Copy
                                     ).then_inc(read, 1)

            def attn1b(t, s):
                bank, read = arrived(act, t, "fc")
                nc.scalar.activation(qat[:, :, :].rearrange("p b i -> p (b i)"), bank[:, :], ACT.Tanh,
                                     bias=fcb[:, 0:1]).then_inc(read, 1)

            def attn2(t, s):
                act.wait_ge(sem("wat_ready"), s + 1)
                nc.scalar.activation(wat[:, :, :], wat[:, :, :], ACT.Exp).then_inc(sem("wat_exp"), 1)

            def attn3(t, s):
                bank, read = arrived(act, t, "tT")
                nc.scalar.activation(xtT[:, :, :].rearrange("p b i -> p (b i)"), bank[:, :], ACT.Copy
                                     ).then_inc(read, 1)

            def attn4(t, s):
                act.wait_ge(sem("pex_ready"), s + 1)
                nc.scalar.activation(pex[:, :, :], pex[:, :, :], ACT.Exp).then_inc(sem("pex_exp"), 1)

            xm_copy(0, None)
            first_tap(0, None)
            silu_x(0)
            qkv(0, None)
            qkv2(0, None)
            qkv3(0, None)

            def silu_z(t):
                for f in range(HALVES):
                    bank, read = arrived(act, t, f"z{f}")
                    nc.scalar.activation(sz[:, f].rearrange("p b i -> p (b i)"), bank[:, :], ACT.Silu
                                         ).then_inc(read, 1)

            def step(t):
                first, last = (isinstance(t, int) and t == 0), (isinstance(t, int) and t == T - 1)
                exps(t, 0)
                if not last:
                    xm_copy(t + 1, t)
                    first_tap(t + 1, t)
                for h in range(1, 4):
                    exps(t, h)
                out_copy(t, 0)
                exps(t, 4)
                exps(t, 5)
                if not first:
                    attn1(t, t - 1)
                exps(t, 6)
                if not first:
                    attn1b(t, t - 1)
                exps(t, 7)
                if not last:
                    act.wait_ge(sem("sx_ready"), t + 1)
                    silu_x(t + 1)
                silu_z(t)
                if not first:
                    attn2(t, t - 1)
                out_copy(t, 1)
                if not last:
                    qkv(t + 1, t)
                    qkv2(t + 1, t)
                if not first:
                    attn3(t, t - 1)
                if not last:
                    qkv3(t + 1, t)
                if not first:
                    attn4(t, t - 1)

            between(act, step)
            attn1(T, T - 1)
            attn1b(T, T - 1)
            attn2(T, T - 1)
            attn3(T, T - 1)
            attn4(T, T - 1)

            def gelu(r, u):
                i = UNROLL * r + u
                act.wait_ge(sem("weights_ready"), i + 1)
                if not (isinstance(r, int) and r == 0 and u < 2):
                    act.wait_ge(sem("result_ready"), i - 1)
                for k in range(FK):
                    if k % 2 == 0:
                        act.wait_ge(sem("hidden_ready"), 2 * i + k // 2 + 1)
                    bank = (pA, pS)[u % 2][k // 2]
                    nc.scalar.activation(hidT[u % 2][:, k, :], bank[:, ROWS * (k % 2):ROWS * (k % 2 + 1)], ACT.Gelu,
                                         bias=b1f[:, u % WBUFS, k:k + 1]
                                         ).then_inc(sem("gelu_done" if k == FK - 1 else "gelu_part"), 1)

            for u in range(UNROLL):
                gelu(0, u)
            with act.Fori(1, ROUNDS) as r:
                for u in range(UNROLL):
                    gelu(r, u)
            for t in range(T):
                act.wait_ge(sem("sum_done"), t + 1)
                act.dma_start(out_d[:, t * P:(t + 1) * P, :].rearrange("b p c -> p b c"),
                              x_tok[:, :, t, :]).then_inc(sem("stored"), 16)
            act.wait_ge(sem("stored"), 16 * T)

        @block.tensor
        def _(pe):
            mm, tr = nc.tensor.matmul, nc.tensor.transpose
            pe.wait_ge(sem("ident_made"), 1)
            for i in range(8):
                bank, written = claim(pe, None, f"x{i}")
                pe.wait_ge(sem(f"x_loaded{i // 2}{i % 2}"), 16)
                for j in range(4):
                    last = tr(bank[:, P * j:P * j + P], x_tok[:, i // 2, 4 * (i % 2) + j, :], ident[:, :])
                last.then_inc(written, 1)
            bank, written = claim(pe, None, "wup")
            pe.wait_ge(sem("matrices_loaded"), 16 * 8)
            for j in range(4):
                last = tr(bank[:, P * j:P * j + P], wup_n[:, j, :], ident[:, :])
            last.then_inc(written, 1)
            bank, written = claim(pe, None, "wdn")
            for j in range(2):
                last = tr(bank[:, P * j:P * j + P], wdn_n[:, P * j:P * j + P], ident[:, :])
            last.then_inc(written, 1)
            bank, written = claim(pe, None, "fcw")
            tr(bank[:, 0:C], fcw_n[:, :], ident[:, :]).then_inc(written, 1)
            pe.wait_ge(sem("bdT_made"), 6)
            for f in range(HALVES):
                bank, written = claim(pe, None, f"bd{f}")
                for w in range(3):
                    last = tr(bank[:, P * w:P * w + P], bdT[:, w, f, :], ident[:, :])
                last.then_inc(written, 1)
            bank, written = claim(pe, None, "gate")
            for j in range(6):
                last = tr(bank[:, 16 * j:16 * j + 16], wg_n[:, P * j:P * j + P], ident[0:16, 0:16])
            last.then_inc(written, 1)
            bank, written = claim(pe, None, "lnT")
            pe.wait_ge(sem("vectors_loaded"), 16 * 20)
            tr(bank[:, 0:2 * E], lngb_n[:, :], ident[0:16, 0:16]).then_inc(written, 1)
            bank, written = claim(pe, None, "gmean")
            pe.wait_ge(sem("gstats_done"), B)
            mm(bank[:, 0:B], avg4[:, :], gmv[:, :, 0], start=True, stop=True).then_inc(written, 1)
            bank, written = claim(pe, None, "gvar")
            pe.wait_ge(sem("gvar_in"), 1)
            mm(bank[:, 0:B], avg4[:, :], gv[:, :], start=True, stop=True).then_inc(written, 1)
            bank, written = claim(pe, None, "geffx")
            taken(pe, None, "gate")
            for f in range(HALVES):
                mm(bank[:, 16 * f:16 * f + 16], bdT[:, 0, f, :], wgT[:, f, :], start=True, stop=False)
                last = mm(bank[:, 16 * f:16 * f + 16], bdT[:, 1, f, :], wgT[:, 2 + f, :], start=False, stop=True)
            last.then_inc(written, 1)
            bank, written = claim(pe, None, "geffm")
            for f in range(HALVES):
                last = mm(bank[:, 16 * f:16 * f + 16], bdT[:, 2, f, :], wgT[:, 4 + f, :], start=True, stop=True)
            last.then_inc(written, 1)
            bank, written = claim(pe, None, "b1")
            for k in range(FK):
                last = tr(bank[:, E * k:E * k + E], b1n[:, P * k:P * k + P], ident[0:E, 0:E])
            last.then_inc(written, 1)

            def up(t, src, lo, names):
                for f in range(HALVES):
                    bank, written = claim(pe, src, names[f])
                    if isinstance(t, int):
                        rhs = xT[:, :, P * t:P * t + P]
                    else:
                        rhs = xT[:, :, bass.ds(t * P, P)]
                    mm(bank[:, :], wupT[:, lo + f, :], rhs, start=True, stop=True).then_inc(written, 1)

            def qkv(t, src):
                pe.wait_ge(sem("xact_ready"), 2 * t + 2)
                if src is None:
                    taken(pe, src, "xm1")
                for b in range(B):
                    bank, written = claim(pe, src, f"k{b}")
                    xmb = [xm[:, f, b, CONV - 1:] for f in range(HALVES)]
                    mm(bank[:, 0:P + 16], xact[:, 0, b, :], kg[:, 0, :], start=True, stop=False, skip_group_check=True)
                    mm(bank[:, P:INNER + 16], xact[:, 1, b, :], kg[:, 1, :], start=False, stop=False,
                       skip_group_check=True)
                    mm(bank[:, P:P + 16], xmb[0], mg[:, 0, :], start=False, stop=False, skip_group_check=True)
                    mm(bank[:, P:P + 16], xmb[1], mg[:, 1, :], start=False, stop=True,
                       skip_group_check=True).then_inc(written, 1)
                    bank, written = claim(pe, src, f"v{b}")
                    for f in range(HALVES):
                        last = mm(bank[:, P * f:P * f + P], xmb[f], bd[:, 2, f, :], start=True, stop=True)
                    last.then_inc(written, 1)

            def qkv2(t, src):
                bank, written = claim(pe, src, "gateT")
                for k in range(2):
                    last = tr(bank[0:BH, P * k:P * k + P], gates[:, k].rearrange("p b h -> p (b h)"), ident[:, :])
                last.then_inc(written, 1)
                for w, names in ((0, ("q0", "q1")), (1, ("kT0", "kT1"))):
                    for f in range(HALVES):
                        bank, written = claim(pe, src, names[f])
                        mm(bank[:, :], bd[:, w, f, :], xact[:, f].rearrange("p b i -> p (b i)"),
                           start=True, stop=True).then_inc(written, 1)

            def qkv3(t, src):
                for f in range(HALVES):
                    bank, written = claim(pe, src, f"uq{f}")
                    pe.wait_ge(sem("uq_ready"), t + 1)
                    for b in range(B):
                        last = mm(bank[:, P * b:P * b + P], spread[:, f, b].rearrange("p h d -> p (h d)"), uq[:, :],
                                  start=True, stop=True)
                    last.then_inc(written, 1)
                bank, written = claim(pe, src, "gtok")
                wait_apart(pe, sem("gm2_done"), 2 * t + 2)
                for k in range(2):
                    last = tr(bank[:, BH * k:BH * k + BH], gm2[:, k, :], ident[0:BH, 0:BH])
                last.then_inc(written, 1)

            def head(t, h):
                f, q = h // HPH, DH * (h % HPH)
                if not (isinstance(t, int) and t == 0 and h < 2):
                    pe.wait_ge(sem("decay_ready"), NH * t + h - 1)
                A = pA[h % 2]
                mm(A[:, :], parts[:, 0, :], bc(pick[:, h, :], 2, P), start=True, stop=False)
                mm(A[:, :], neghead[:, h:h + 1].broadcast_to([96, P]), cexp[:, :, :].rearrange("p b i -> p (b i)"),
                   start=False, stop=False)
                mm(A[:, :], ident_b[:, :], maskneg[:, :, :].rearrange("p b i -> p (b i)"), start=False,
                   stop=True).then_inc(sem("exponents_ready"), 1)
                if not (isinstance(t, int) and t == 0 and h < 2):
                    pe.wait_ge(sem("weighted"), NH * t + h - 1)
                for b in range(B):
                    last = mm(pS[h % 2][:, P * b:P * b + P], kT[q:q + DH, f, b, :], qT[q:q + DH, f, b, :],
                              start=True, stop=True)
                last.then_inc(sem("scores_ready"), 1)

            def from_state(t, f):
                if not (isinstance(t, int) and t == 0 and f == 0):
                    pe.wait_ge(sem("half_copied"), 4 * t + 2 * f)
                for b in range(B):
                    mm(pO[b // 2][:, (b % 2) * HPH * DE:(b % 2 + 1) * HPH * DE], qpT[:, f, b, :],
                       KVm[:, f * B + b, :], start=(b % 2 == 0), stop=False, skip_group_check=True)

            def values(t, h):
                pe.wait_ge(sem("weighted"), NH * t + h + 1)
                for b in range(B):
                    o = (b % 2) * HPH * DE + (h % HPH) * DE
                    last = mm(pO[b // 2][:, o:o + DE], PT[:, h % 2, b, :], vext[:, b, h, :], start=False,
                              stop=(h % HPH == HPH - 1), skip_group_check=True)
                if h % HPH == HPH - 1:
                    last.then_inc(sem("half_ready"), 1)

            def state(t):
                pe.wait_ge(sem("vs_ready"), t + 1)
                for b in range(B):
                    bank = (pA + pS)[b]
                    for f in range(HALVES):
                        last = mm(bank[:, f * HPH * DE:(f + 1) * HPH * DE], ktok[:, b, P * f:P * f + P],
                                  vs[:, b, HPH * f:HPH * f + HPH, :].rearrange("p h d -> p (h d)"),
                                  start=True, stop=True)
                last.then_inc(sem("state_summed"), 1)

            def attn1(t, s):
                bank, written = claim(pe, t, "hnT")
                pe.wait_ge(sem("h1_ready"), B * s + B)
                for b in range(B):
                    last = tr(bank[:, P * b:P * b + P], hnm[:, b, :], ident[:, :])
                last.then_inc(written, 1)

            def attn1b(t, s):
                bank, written = claim(pe, t, "fc")
                taken(pe, t, "hnT")
                mm(bank[:, :], fcwT[:, :], hnmT[:, :, :].rearrange("p b i -> p (b i)"), start=True,
                   stop=True).then_inc(written, 1)

            def attn2(t, s):
                bank, written = claim(pe, t, "score")
                taken(pe, t, "fc")
                for b in range(B):
                    last = mm(bank[:, b:b + 1], qat[:, b, :], scw[:, :], start=True, stop=True)
                last.then_inc(written, 1)

            def attn3(t, s):
                bank, written = claim(pe, t, "tT")
                pe.wait_ge(sem("xt_ready"), B * s + B)
                for b in range(B):
                    last = tr(bank[:, P * b:P * b + P], xt[:, b, :], ident[:, :])
                last.then_inc(written, 1)

            def attn3b(t, s):
                bank, written = claim(pe, t, "logit")
                taken(pe, t, "tT")
                for b in range(B):
                    last = mm(bank[:, E * b:E * b + E], xtT[:, b, :], wr[:, :], start=True, stop=True)
                last.then_inc(written, 1)

            def attn4(t, s, name="count"):
                bank, written = claim(pe, t, name)
                pe.wait_ge(sem("sel_ready"), s + 1)
                mm(bank[:, 0:B * E], before[:, :], selb[:, :, :].rearrange("p b e -> p (b e)"), start=True,
                   stop=False, skip_group_check=True)
                for b in range(B):
                    for b2 in range(b + 1, B):
                        mm(bank[:, E * b2:E * b2 + E], ones_b[:, :], selb[:, b, :], start=False, stop=False,
                           skip_group_check=True)
                    last = mm(bank[:, B * E:B * E + E], ones_b[:, :], selb[:, b, :], start=False, stop=(b == B - 1),
                              skip_group_check=True)
                last.then_inc(written, 1)

            def turn_heads(t, s):
                for f in range(HALVES):
                    bank, written = claim(pe, t, f"y{f}")
                    pe.wait_ge(sem("hn_ready"), 2 * s + f + 1)
                    for b in range(B):
                        last = tr(bank[:, P * b:P * b + P],
                                  hn[:, b, HPH * f:HPH * f + HPH, :].rearrange("p h d -> p (h d)"), ident[:, :])
                    last.then_inc(written, 1)

            def down(t, s):
                for k in range(2):
                    bank, written = claim(pe, t, f"down{k}")
                    pe.wait_ge(sem("y_ready"), 2 * s + 2)
                    for b in range(2):
                        for f in range(HALVES):
                            last = mm(bank[:, P * b:P * b + P], yT[:, f, 2 * k + b, :], wdnT[:, f, :],
                                      start=(f == 0), stop=(f == 1))
                    last.then_inc(written, 1)

            pe.wait_ge(sem("xn_ready"), B)
            pe.wait_ge(sem("gate_weights_made"), 1)
            pe.wait_ge(sem("pool_tables_made"), 1)
            up(0, None, 0, ("xm0", "xm1"))
            qkv(0, None)
            qkv2(0, None)
            qkv3(0, None)

            def begin(t):
                pe.wait_ge(sem("parts_ready"), t + 1)
                if not (isinstance(t, int) and t == 0):
                    pe.wait_ge(sem("state_taken"), HALVES * B * t)
                head(t, 0)

            def step(t):
                first, last = (isinstance(t, int) and t == 0), (isinstance(t, int) and t == T - 1)
                if first:
                    begin(0)
                if not last:
                    up(t + 1, t, 0, ("xm0", "xm1"))
                head(t, 1)
                pe.wait_ge(sem("qp_ready"), 2 * t + 2)
                pe.wait_ge(sem("state_ready"), t + 1)
                from_state(t, 0)
                values(t, 0)
                head(t, 2)
                values(t, 1)
                if not first:
                    turn_heads(t, t - 1)
                head(t, 3)
                values(t, 2)
                if not first:
                    down(t, t - 1)
                values(t, 3)
                head(t, 4)
                head(t, 5)
                from_state(t, 1)
                values(t, 4)
                if not first:
                    attn1(t, t - 1)
                head(t, 6)
                values(t, 5)
                if not first:
                    attn1b(t, t - 1)
                head(t, 7)
                values(t, 6)
                if not first:
                    attn2(t, t - 1)
                up(t, t, 2, ("z0", "z1"))
                values(t, 7)
                if not last:
                    pe.wait_ge(sem("decay_ready"), NH * t + NH)
                    state(t)
                    qkv(t + 1, t)
                    qkv2(t + 1, t)
                if not first:
                    attn3(t, t - 1)
                    attn3b(t, t - 1)
                if not last:
                    qkv3(t + 1, t)
                if not last:
                    begin(t + 1)
                if not first and not last:
                    attn4(t, t - 1)

            between(pe, step)
            turn_heads(T, T - 1)
            down(T, T - 1)
            attn1(T, T - 1)
            attn1b(T, T - 1)
            attn4(T, T - 2, "count_before")
            attn2(T, T - 1)
            attn3(T, T - 1)
            attn3b(T, T - 1)
            attn4(T, T - 1)

            def turn_in(r, u):
                pe.wait_ge(sem(f"rows_loaded{u}"), 16 * (r + 1))
                if not (isinstance(r, int) and r == 0 and u < 2):
                    pe.wait_ge(sem("inputs_ready"), UNROLL * r + u - 1)
                for j in range(SUBS):
                    last = tr(pG[u % 2][:, P * j:P * j + P], xin[u // 4][:, u % 4, j, 0:C], ident[:, :])
                last.then_inc(sem("rows_turned"), 1)

            def hidden(r, u):
                i = UNROLL * r + u
                pe.wait_ge(sem("inputs_ready"), i + 1)
                if not (isinstance(r, int) and r == 0 and u < 2):
                    pe.wait_ge(sem("gelu_done"), i - 1)
                for k in range(FK):
                    bank = (pA, pS)[u % 2][k // 2]
                    last = mm(bank[:, ROWS * (k % 2):ROWS * (k % 2 + 1)], w1f[u % WBUFS][:, P * k:P * k + P],
                              xeT[:, u % WBUFS, :], start=True, stop=True)
                    if k % 2 == 1:
                        last.then_inc(sem("hidden_ready"), 1)

            def result(r, u):
                i = UNROLL * r + u
                pe.wait_ge(sem("gelu_done"), i + 1)
                if not (isinstance(r, int) and r == 0 and u < 2):
                    pe.wait_ge(sem("y_weighted"), i - 1)
                for j in range(SUBS):
                    o = pO[u % 2][:, C * j:C * j + C]
                    for k in range(FK):
                        mm(o, hidT[u % 2][:, k, P * j:P * j + P], w2f[u % WBUFS][:, C * k:C * k + C], start=(k == 0),
                           stop=False)
                    last = mm(o, ones_b[0:3, :], b2f[:, u % WBUFS, :], start=False, stop=True)
                last.then_inc(sem("result_ready"), 1)

            def round_(r, more):
                for u in range(UNROLL):
                    if u + 2 < UNROLL:
                        turn_in(r, u + 2)
                    elif more:
                        turn_in(r + 1, u + 2 - UNROLL)
                    hidden(r, u)
                    if u > 0:
                        result(r, u - 1)
                    elif not (isinstance(r, int) and r == 0):
                        result(r - 1, UNROLL - 1)

            turn_in(0, 0)
            turn_in(0, 1)
            round_(0, True)
            with pe.Fori(1, ROUNDS - 1) as r:
                round_(r, True)
            round_(ROUNDS - 1, False)
            result(ROUNDS - 1, UNROLL - 1)

        @block.vector
        def _(dve):
            v = nc.vector
            made = [0]

            def chain(ins):
                made[0] += 1
                ins.then_inc(sem("dve_chain"), 1)
                dve.wait_ge(sem("dve_chain"), made[0])

            chain(v.memset(lcar[:, :], 0.0))
            chain(v.memset(xm[:, :, :, :], 0.0))
            chain(v.memset(vext[:, :, :, :], 1.0))
            chain(v.memset(KV[:, :, :], 0.0))
            chain(v.memset(mhalf[:, :], -0.5))
            chain(v.memset(eones[:, :], 1.0))
            v.memset(KVm[:, :, :], 0.0).then_inc(sem("state_ready"), 1)
            for i in range(8):
                bank, n = use(None, f"x{i}")
                dve.wait_ge(sem(f"general{bank}_read"), n + 1)
                v.bn_stats(gst[:, i // 2, i % 2, :], xT[:, i // 2, 512 * (i % 2):512 * (i % 2) + 512]
                           ).then_inc(sem("gst_done"), 1)
            for b in range(B):
                dve.wait_ge(sem("gst_done"), 2 * b + 2)
                v.bn_aggr(gmv[:, b, :], gst[:, b, :, :].rearrange("p k s -> p (k s)")).then_inc(sem("gstats_done"), 1)
            dve.wait_ge(sem("matrices_loaded"), 16 * 8)
            dve.wait_ge(sem("block4_made"), 1)
            for w in range(3):
                for f in range(HALVES):
                    v.tensor_tensor(bdT[:, w, f, :].rearrange("p (n d) -> p n d", d=4),
                                    block4[:, :].rearrange("p (n d) -> p n d", d=4),
                                    bc(wqkv_n[:, w, f, :], 1, 32), ALU.mult).then_inc(sem("bdT_made"), 1)
            for f in range(HALVES):
                bank, read = arrived(dve, None, f"bd{f}")
                v.tensor_copy(bd[:, :, f, :], bank[:, 0:3 * P].rearrange("p (w c) -> p w c", w=3)).then_inc(read, 1)
            bank, read = arrived(dve, None, "gate")
            v.tensor_copy(wgT[:, :, :].rearrange("p j g -> p (j g)"), bank[:, 0:96]).then_inc(read, 1)
            bank, read = arrived(dve, None, "lnT")
            v.tensor_copy(lngbT[:, :], bank[:, 0:2 * E]).then_inc(read, 1)
            bank, read = arrived(dve, None, "gmean")
            v.tensor_copy(gm[:, :], bank[:, 0:B]).then_inc(read, 1)
            taken(dve, None, "gmean")
            chain(v.tensor_tensor(gd[:, :], gmv[:, :, 0], gm[:, :], ALU.subtract))
            chain(v.tensor_tensor(gd[:, :], gd[:, :], gd[:, :], ALU.mult))
            v.tensor_tensor(gv[:, :], gd[:, :], gmv[:, :, 1], ALU.add).then_inc(sem("gvar_in"), 1)
            bank, read = arrived(dve, None, "gvar")
            v.tensor_scalar(gr[:, :], bank[:, 0:B], GN_EPS, None, ALU.add).then_inc(read, 1)
            dve.wait_ge(sem("gr_done"), 1)
            for b in range(B):
                v.tensor_scalar(xT[:, b, :], xT[:, b, :], gm[:, b:b + 1], gr[:, b:b + 1], ALU.subtract, ALU.mult
                                ).then_inc(sem("xn_ready"), 1)
            bank, read = arrived(dve, None, "geffx")
            chain(v.tensor_copy(kg[:, 0, P:P + 16], bank[:, 0:16]))
            v.tensor_copy(kg[:, 1, 0:16], bank[:, 16:32]).then_inc(read, 1)
            bank, read = arrived(dve, None, "geffm")
            v.tensor_copy(mg[:, :, :].rearrange("p f g -> p (f g)"), bank[:, 0:32]).then_inc(read, 1)
            taken(dve, None, "geffm")
            taken(dve, None, "bd0")
            taken(dve, None, "bd1")
            chain(v.tensor_copy(kg[:, 0, 0:P], bd[:, 1, 0, :]))
            v.tensor_copy(kg[:, 1, 16:P + 16], bd[:, 1, 1, :]).then_inc(sem("gate_weights_made"), 1)
            bank, read = arrived(dve, None, "b1")
            v.tensor_copy(b1T[:, :, :].rearrange("p k e -> p (k e)"), bank[:, 0:FK * E]).then_inc(read, 1)
            for k in range(3):
                if k < 2:
                    chain(v.tensor_copy(bparts[:, k, :], b2n[:, :]))
                    chain(v.tensor_tensor(b2n[:, :], b2n[:, :], bparts[:, k, :], ALU.subtract))
                else:
                    v.tensor_copy(bparts[:, k, :], b2n[:, :]).then_inc(sem("bparts_made"), 1)

            def halo(t, f):
                if isinstance(t, int) and t == 0:
                    v.memset(xm[:, f, :, 0:CONV - 1], 0.0).then_inc(sem("halo_moved"), 1)
                else:
                    dve.wait_ge(sem("conv_done"), 2 * t - 1 + f)
                    v.tensor_copy(xm[:, f, :, 0:CONV - 1], xm[:, f, :, P:P + CONV - 1]).then_inc(sem("halo_moved"), 1)

            def conv(t, src, halves=range(HALVES)):
                for f in halves:
                    dve.wait_ge(sem("tap0_done"), 2 * t + f + 1)
                    for k in range(1, CONV):
                        if k > 1:
                            dve.wait_ge(sem("tap_done"), (2 * t + f) * (CONV - 2) + k - 1)
                        v.scalar_tensor_tensor(cacc[:, f], xm[:, f, :, k:k + P], convw[:, f, k:k + 1], cacc[:, f],
                                               ALU.mult, ALU.add
                                               ).then_inc(sem("tap_done" if k < CONV - 1 else "conv_done"), 1)

            def gate(t, src):
                taken(dve, src, "gateT")
                if isinstance(t, int) and t == 0:
                    v.memset(rcar[:, 0:1], NEG).then_inc(sem("gate_chain"), 1)
                else:
                    v.tensor_copy(rcar[:, 0:1], gc[:, 1, P - 1:P]).then_inc(sem("gate_chain"), 1)
                v.tensor_scalar(fmin[:, :], gpre[:, 1, :], 0.0, None, ALU.min
                                ).then_inc(sem("gate_chain"), 1)
                dve.wait_ge(sem("fln_done"), t + 1)
                dve.wait_ge(sem("gate_chain"), 10 * t + 2)
                v.tensor_tensor_scan(lc[:, :], fmin[:, :], fabs[:, :], lcar[:, 0:1], ALU.add, ALU.subtract
                                     ).then_inc(sem("gate_chain"), 1)
                dve.wait_ge(sem("gate_chain"), 10 * t + 3)
                v.tensor_copy(lcar[:, :], lc[:, P - 1:P]).then_inc(sem("gate_chain"), 1)
                v.tensor_tensor(gc[:, 0, :], gpre[:, 0, :], lc[:, :], ALU.subtract).then_inc(sem("g_done"), 1)
                dve.wait_ge(sem("g_done"), t + 1)
                dve.wait_ge(sem("gate_chain"), 10 * t + 4)
                v.tensor_tensor_scan(gc[:, 1, :], gc[:, 0, :], gc[:, 0, :], rcar[:, 0:1], ALU.max, ALU.max
                                     ).then_inc(sem("c_ready"), 1)
                dve.wait_ge(sem("c_ready"), t + 1)
                v.tensor_scalar(rcar[:, 1:2], gc[:, 1, P - 1:P], -1.0, None, ALU.mult).then_inc(sem("r_end_ready"), 1)
                v.tensor_tensor(fmin[:, :], lc[:, :], gc[:, 1, :], ALU.add).then_inc(sem("m_ready"), 1)
                v.tensor_copy(parts[0:BH], gc[:, :, :]).then_inc(sem("gate_chain"), 1)
                dve.wait_ge(sem("gate_chain"), 10 * t + 5)
                v.tensor_tensor(r1[:, :, :], gc[:, :, :], parts[0:BH], ALU.subtract).then_inc(sem("gate_chain"), 1)
                dve.wait_ge(sem("gate_chain"), 10 * t + 6)
                v.tensor_copy(parts[BH:2 * BH], r1[:, :, :]).then_inc(sem("gate_chain"), 1)
                v.tensor_copy(gmid[:, :, :], r1[:, :, :]).then_inc(sem("gate_chain"), 1)
                dve.wait_ge(sem("gate_chain"), 10 * t + 8)
                v.tensor_tensor(r2[:, :, :], r1[:, :, :], gmid[:, :, :], ALU.subtract).then_inc(sem("gate_chain"), 1)
                dve.wait_ge(sem("gate_chain"), 10 * t + 9)
                v.tensor_copy(parts[2 * BH:3 * BH], r2[:, :, :]).then_inc(sem("gate_chain"), 1)
                dve.wait_ge(sem("gate_chain"), 10 * t + 10)
                v.tensor_tensor(cexp[:, :, :], bc(parts[:, 1, :], 1, B), bc(ofbatch[:, :], 2, P), ALU.mult
                                ).then_inc(sem("parts_ready"), 1)

            def qprime(t, src):
                for f in range(HALVES):
                    bank, read = arrived(dve, src, f"uq{f}")
                    taken(dve, src, f"q{f}")
                    v.tensor_tensor(qpT[:, f].rearrange("p b i -> p (b i)"), qT[:, f].rearrange("p b i -> p (b i)"),
                                    bank[:, :], ALU.mult).then_inc(sem("qp_ready"), 1)
                    v.tensor_copy(decay[:, f, :], bank[:, :].rearrange("p (b i) -> p b i", b=B)[:, :, P - 1]
                                  ).then_inc(read, 1)

            def weigh(t, h):
                dve.wait_ge(sem("decay_ready"), NH * t + h + 1)
                dve.wait_ge(sem("scores_ready"), NH * t + h + 1)
                v.tensor_tensor(PT[:, h % 2].rearrange("p b i -> p (b i)"), pS[h % 2][:, :],
                                D[:, h % 2].rearrange("p b i -> p (b i)"), ALU.mult).then_inc(sem("weighted"), 1)

            def new_state(t):
                dve.wait_ge(sem("state_summed"), t + 1)
                for b in range(B):
                    for f in range(HALVES):
                        v.scalar_tensor_tensor(KV[:, f * B + b, :], KV[:, f * B + b, :], decay[:, f, b:b + 1],
                                               (pA + pS)[b][:, f * HPH * DE:(f + 1) * HPH * DE],
                                               ALU.mult, ALU.add).then_inc(sem("state_taken"), 1)

            def norm_a(t, f):
                o, num = osb[:, f], osb[:, f, :, :, 0:DH]
                dve.wait_ge(sem("half_copied"), 4 * t + 2 * f + 2)
                expm = gtok[:, 1, :, HPH * f:HPH * f + HPH]
                v.scalar_tensor_tensor(nrm[:, f], o[:, :, :, DH], -1.0, expm, ALU.mult, ALU.max
                                       ).then_inc(sem("norm_taken"), 1)
                v.tensor_reduce(mu[:, f], num, AX.X, ALU.add).then_inc(sem("norm_chain"), 1)
                dve.wait_ge(sem("norm_taken"), 2 * t + f + 1)
                v.tensor_tensor(nrm[:, f], nrm[:, f], o[:, :, :, DH], ALU.max).then_inc(sem("norm_chain"), 1)
                dve.wait_ge(sem("norm_chain"), 8 * (2 * t + f) + 2)
                v.tensor_scalar(nrm[:, f], nrm[:, f], ROW_EPS, None, ALU.add).then_inc(sem("norm_chain"), 1)
                v.tensor_scalar(mu[:, f], mu[:, f], 1.0 / DH, None, ALU.mult).then_inc(sem("norm_chain"), 1)
                dve.wait_ge(sem("norm_chain"), 8 * (2 * t + f) + 3)
                v.reciprocal(rr[:, f], nrm[:, f]).then_inc(sem("norm_chain"), 1)
                dve.wait_ge(sem("norm_chain"), 8 * (2 * t + f) + 4)
                v.tensor_tensor(dd[:, f].rearrange("p b h d -> p (b h) d"), num.rearrange("p b h d -> p (b h) d"),
                                bc(mu[:, f].rearrange("p b h -> p (b h)"), 2, DH), ALU.subtract
                                ).then_inc(sem("norm_read"), 1)

            def norm_b(t, f):
                dve.wait_ge(sem("dsq_done"), 2 * t + f + 1)
                v.tensor_reduce(var[:, f], dsq[:, f], AX.X, ALU.add).then_inc(sem("norm_chain"), 1)
                dve.wait_ge(sem("norm_chain"), 8 * (2 * t + f) + 6)
                v.tensor_tensor(var[:, f], var[:, f], rr[:, f], ALU.mult).then_inc(sem("norm_chain"), 1)
                dve.wait_ge(sem("norm_chain"), 8 * (2 * t + f) + 7)
                v.tensor_tensor(var[:, f], var[:, f], rr[:, f], ALU.mult).then_inc(sem("norm_chain"), 1)
                dve.wait_ge(sem("norm_chain"), 8 * (2 * t + f) + 8)
                v.tensor_scalar(var[:, f], var[:, f], 1.0 / DH, LN_EPS, ALU.mult, ALU.add).then_inc(sem("var_c"), 1)

            def norm2(t, f):
                dve.wait_ge(sem("rstd_ready"), 2 * t + f + 1)
                v.tensor_tensor(rr[:, f], rr[:, f], var[:, f], ALU.mult).then_inc(sem("scale_done"), 1)
                dve.wait_ge(sem("scale_done"), 2 * t + f + 1)
                v.tensor_tensor(hn[:, :, HPH * f:HPH * f + HPH, :], dd[:, f], bc(rr[:, f], 3, DH), ALU.mult
                                ).then_inc(sem("hn_ready"), 1)

            def gated(t, s, f):
                bank, read = arrived(dve, t, f"y{f}")
                dve.wait_ge(sem("sx_ready"), s + 1)
                y = yT[:, f].rearrange("p b i -> p (b i)")
                v.scalar_tensor_tensor(y, bank[:, :], vecs[:, 1, f:f + 1], sx[:, f].rearrange("p b i -> p (b i)"),
                                       ALU.mult, ALU.add).then_inc(read, 1)
                taken(dve, t, f"y{f}")
                v.tensor_tensor(y, y, sz[:, f].rearrange("p b i -> p (b i)"), ALU.mult).then_inc(sem("y_ready"), 1)

            def row(t, b):
                if isinstance(t, int):
                    return x_tok[:, b, t, :]
                return x_tok[:, b, bass.ds(t, 1), :].rearrange("p a c -> p (a c)")

            def xtok(t, k):
                if isinstance(t, int):
                    return x_tok[:, 2 * k:2 * k + 2, t, :]
                return x_tok[:, 2 * k:2 * k + 2, bass.ds(t, 1), :].rearrange("p b a c -> p b (a c)")

            def residual(t, s):
                for k in range(2):
                    bank, read = arrived(dve, t, f"down{k}")
                    v.tensor_tensor(x1[:, 2 * k:2 * k + 2, :], xtok(s, k), bank[:, 0:2 * C].rearrange(
                        "p (b c) -> p b c", b=2), ALU.add).then_inc(read, 1)
                taken(dve, t, "down0")
                taken(dve, t, "down1")
                for b in range(B):
                    v.bn_stats(st1[:, b, :], x1[:, b, :]).then_inc(sem("residual_chain"), 1)
                for b in range(B):
                    wait_apart(dve, sem("residual_chain"), 2 * B * s + b + 1)
                    v.bn_aggr(mv1[:, b, :], st1[:, b, :]).then_inc(sem("residual_chain"), 1)
                dve.wait_ge(sem("residual_chain"), 2 * B * s + 2 * B)
                v.tensor_scalar(rs1[:, :], mv1[:, :, 1], LN_EPS, None, ALU.add).then_inc(sem("var1_ready"), 1)

            def attn1(t, s):
                dve.wait_ge(sem("rs1_ready"), s + 1)
                for b in range(B):
                    v.tensor_scalar(hnm[:, b, :], x1[:, b, :], mv1[:, b, 0:1], rs1[:, b:b + 1], ALU.subtract,
                                    ALU.mult).then_inc(sem("h1_ready"), 1)

            def attn2(t, s):
                bank, read = arrived(dve, t, "score")
                v.tensor_copy(esc[:, :], bank[:, 0:B]).then_inc(read, 1)
                taken(dve, t, "score")
                v.tensor_tensor_scan(emax[:, :], esc[:, :], esc[:, :], NEG, ALU.max, ALU.max
                                     ).then_inc(sem("softmax_chain"), 1)
                dve.wait_ge(sem("softmax_chain"), 6 * s + 1)
                v.tensor_tensor(wat[:, :, :], bc(esc[:, :], 1, B), bc(emax[:, :], 2, B), ALU.subtract
                                ).then_inc(sem("softmax_chain"), 1)
                dve.wait_ge(sem("softmax_chain"), 6 * s + 2)
                v.tensor_scalar(wat[:, :, :], wat[:, :, :], 0.0, None, ALU.min).then_inc(sem("wat_ready"), 1)

            def attn3(t, s):
                dve.wait_ge(sem("wat_exp"), s + 1)
                v.tensor_tensor(wat[:, :, :], wat[:, :, :], causal4[:, :, :], ALU.mult
                                ).then_inc(sem("softmax_chain"), 1)
                dve.wait_ge(sem("softmax_chain"), 6 * s + 3)
                v.tensor_reduce(wsum[:, :], wat[:, :, :], AX.X, ALU.add).then_inc(sem("softmax_chain"), 1)
                dve.wait_ge(sem("softmax_chain"), 6 * s + 4)
                v.reciprocal(wsum[:, :], wsum[:, :]).then_inc(sem("softmax_chain"), 1)
                dve.wait_ge(sem("softmax_chain"), 6 * s + 5)
                v.tensor_tensor(wat[:, :, :], wat[:, :, :], bc(wsum[:, :], 2, B), ALU.mult
                                ).then_inc(sem("softmax_chain"), 1)
                dve.wait_ge(sem("softmax_chain"), 6 * s + 6)
                for k in range(B):
                    for b in range(k, B):
                        if k > 0:
                            dve.wait_ge(sem("mixed"), 10 * s + sum(B - j for j in range(k - 1)) + (b - k + 1) + 1)
                        v.scalar_tensor_tensor(row(s, b), hnm[:, k, :], wat[:, b, k:k + 1],
                                               x1[:, b, :] if k == 0 else row(s, b), ALU.mult, ALU.add
                                               ).then_inc(sem("mixed"), 1)
                wait_apart(dve, sem("mixed"), 10 * s + 10)
                for b in range(B):
                    v.bn_stats(st3[:, b, :], row(s, b)).then_inc(sem("stats3_chain"), 1)
                for b in range(B):
                    wait_apart(dve, sem("stats3_chain"), 2 * B * s + b + 1)
                    v.bn_aggr(mv3[:, b, :], st3[:, b, :]).then_inc(sem("stats3_chain"), 1)
                dve.wait_ge(sem("stats3_chain"), 2 * B * s + 2 * B)
                v.tensor_scalar(rs3[:, :], mv3[:, :, 1], LN_EPS, None, ALU.add).then_inc(sem("var3_ready"), 1)

            def attn4(t, s):
                dve.wait_ge(sem("rs3_ready"), s + 1)
                for b in range(B):
                    v.tensor_scalar(xt[:, b, :], row(s, b), mv3[:, b, 0:1], rs3[:, b:b + 1], ALU.subtract,
                                    ALU.mult).then_inc(sem("xt_ready"), 1)
                v.tensor_tensor(v2[:, :], rs3[:, :], rs3[:, :], ALU.mult).then_inc(sem("variance_chain"), 1)
                dve.wait_ge(sem("variance_chain"), 2 * s + 1)
                v.tensor_tensor(v2[:, :], v2[:, :], mv3[:, :, 1], ALU.mult).then_inc(sem("variance_chain"), 1)
                dve.wait_ge(sem("variance_chain"), 2 * s + 2)
                v.tensor_scalar(v2[:, :], v2[:, :], LN_EPS, None, ALU.add).then_inc(sem("v2_ready"), 1)

            def attn5(t, s):
                bank, read = arrived(dve, t, "logit")
                v.tensor_tensor(lg[:, :, :], bank[:, 0:B * E].rearrange("p (b e) -> p b e", b=B), bc(brb[:, :], 1, B),
                                ALU.add).then_inc(read, 1)
                taken(dve, t, "logit")
                v.tensor_reduce(lmax[:, :], lg[:, :, :], AX.X, ALU.max).then_inc(sem("rank_chain"), 1)
                other = bc(lg[:, :, :], 2, E)
                own = bc(lg[:, :, :], 3, E)
                v.tensor_tensor(cmp[:, :, :, :], other, own, ALU.is_gt).then_inc(sem("rank_chain"), 1)
                v.tensor_tensor(ceq[:, :, :, :], other, own, ALU.is_equal).then_inc(sem("rank_chain"), 1)
                dve.wait_ge(sem("rank_chain"), 6 * s + 1)
                v.tensor_tensor(pex[:, :, :], lg[:, :, :], bc(lmax[:, :], 2, E), ALU.subtract
                                ).then_inc(sem("pex_ready"), 1)
                dve.wait_ge(sem("rank_chain"), 6 * s + 3)
                v.tensor_tensor(ceq[:, :, :, :].rearrange("p b e f -> p b (e f)"),
                                ceq[:, :, :, :].rearrange("p b e f -> p b (e f)"),
                                bc(lower8[:, :, :].rearrange("p e f -> p (e f)"), 1, B), ALU.mult
                                ).then_inc(sem("rank_chain"), 1)
                dve.wait_ge(sem("rank_chain"), 6 * s + 4)
                v.tensor_tensor(cmp[:, :, :, :], cmp[:, :, :, :], ceq[:, :, :, :], ALU.add
                                ).then_inc(sem("rank_chain"), 1)
                dve.wait_ge(sem("rank_chain"), 6 * s + 5)
                v.tensor_reduce(rank[:, :, :], cmp[:, :, :, :], AX.X, ALU.add).then_inc(sem("rank_chain"), 1)
                dve.wait_ge(sem("rank_chain"), 6 * s + 6)
                for k in range(2):
                    v.tensor_scalar(oh[:, k], rank[:, :, :], float(k), None, ALU.is_equal).then_inc(sem("oh_done"), 1)
                v.tensor_scalar(selb[:, :, :], rank[:, :, :], 1.5, None, ALU.is_lt).then_inc(sem("sel_ready"), 1)

            def attn6(t, s, name="count"):
                bank, read = arrived(dve, t, name)
                v.tensor_tensor(pos[:, :, :], bank[:, 0:B * E].rearrange("p (b e) -> p b e", b=B),
                                bc(offs[:, :], 1, B), ALU.add).then_inc(sem("route_chain"), 1)
                dve.wait_ge(sem("route_chain"), 7 * s + 1)
                v.tensor_tensor(offs[:, :], offs[:, :], bank[:, B * E:B * E + E], ALU.add).then_inc(read, 1)
                dve.wait_ge(sem("pex_exp"), s + 1)
                dve.wait_ge(sem("oh_done"), 2 * s + 2)
                v.tensor_tensor(tmpk[:, :, :, :].rearrange("p k b e -> p k (b e)"),
                                oh[:, :, :, :].rearrange("p k b e -> p k (b e)"),
                                bc(pex[:, :, :].rearrange("p b e -> p (b e)"), 1, 2), ALU.mult
                                ).then_inc(sem("route_chain"), 1)
                dve.wait_ge(sem("route_chain"), 7 * s + 2)
                v.tensor_reduce(wk[:, :, :], tmpk[:, :, :, :], AX.X, ALU.add).then_inc(sem("route_chain"), 1)
                dve.wait_ge(sem("route_chain"), 7 * s + 3)
                v.tensor_tensor(wks[:, :], wk[:, 0, :], wk[:, 1, :], ALU.add).then_inc(sem("route_chain"), 1)
                dve.wait_ge(sem("route_chain"), 7 * s + 4)
                v.reciprocal(wks[:, :], wks[:, :]).then_inc(sem("route_chain"), 1)
                if not (isinstance(s, int) and s == 0):
                    for k in range(2):
                        for b in range(B):
                            dve.wait_ge(sem(f"scattered{k}{b}"), 16 * s)
                dve.wait_ge(sem("route_chain"), 7 * s + 5)
                v.tensor_tensor(xrow[:, :, :, C].rearrange("p b k -> p k b"), wk[:, :, :], bc(wks[:, :], 1, 2),
                                ALU.mult).then_inc(sem("row_part"), 1)
                v.tensor_copy(xrow[:, :, :, C + 1].bitcast(I32), dest[:, :, :]).then_inc(sem("row_part"), 1)
                dve.wait_ge(sem("row_part"), (2 + B) * s + 2)
                v.tensor_scalar(dest[:, :, :], dest[:, :, :], float(P), None, ALU.add)
                dve.wait_ge(sem("rs4_ready"), s + 1)
                for b in range(B):
                    v.tensor_scalar(xrow[:, b, :, 0:C], bc(xt[:, b, :], 1, 2), rs4[:, b:b + 1], None, ALU.mult
                                    ).then_inc(sem("row_part"), 1)
                v.tensor_tensor(tmpk[:, :, :, :].rearrange("p k b e -> p k (b e)"),
                                oh[:, :, :, :].rearrange("p k b e -> p k (b e)"),
                                bc(pos[:, :, :].rearrange("p b e -> p (b e)"), 1, 2), ALU.mult
                                ).then_inc(sem("route_chain"), 1)
                dve.wait_ge(sem("route_chain"), 7 * s + 6)
                v.tensor_reduce(slotf[:, :, :], tmpk[:, :, :, :], AX.X, ALU.add).then_inc(sem("route_chain"), 1)
                dve.wait_ge(sem("route_chain"), 7 * s + 7)
                v.tensor_copy(slot[:, :, :], slotf[:, :, :]).then_inc(sem("slots_ready"), 1)

            dve.wait_ge(sem("pool_tables_made"), 1)
            for f in range(HALVES):
                halo(0, f)
            conv(0, None)
            for f in range(HALVES):
                halo(1, f)
            gate(0, None)
            qprime(0, None)
            dve.wait_ge(sem("b2p_made"), 48)
            chain(v.tensor_copy(offs[:, :], region0[:, :]))

            def step(t):
                first, last = (isinstance(t, int) and t == 0), (isinstance(t, int) and t == T - 1)
                weigh(t, 0)
                if not first:
                    norm2(t - 1, 0)
                    norm2(t - 1, 1)
                weigh(t, 1)
                weigh(t, 2)
                if not first:
                    gated(t, t - 1, 0)
                    gated(t, t - 1, 1)
                weigh(t, 3)
                if not last:
                    conv(t + 1, t, [0])
                    halo(t + 2, 0)
                if not first:
                    residual(t, t - 1)
                weigh(t, 4)
                weigh(t, 5)
                if not first:
                    attn1(t, t - 1)
                if not last:
                    conv(t + 1, t, [1])
                    halo(t + 2, 1)
                weigh(t, 6)
                norm_a(t, 0)
                weigh(t, 7)
                if not first:
                    attn2(t, t - 1)
                norm_b(t, 0)
                if not last:
                    new_state(t)
                norm_a(t, 1)
                if not first:
                    attn3(t, t - 1)
                if last:
                    norm_b(t, 1)
                    attn4(t, t - 1)
                    return
                if not first:
                    attn4(t, t - 1)
                gate(t + 1, t)
                if not first:
                    attn5(t, t - 1)
                qprime(t + 1, t)
                norm_b(t, 1)
                if not first:
                    attn6(t, t - 1)

            between(dve, step)
            for f in range(HALVES):
                norm2(T - 1, f)
            attn5(T - 1, T - 2)
            for f in range(HALVES):
                gated(T, T - 1, f)
            residual(T, T - 1)
            attn1(T, T - 1)
            attn6(T, T - 2, "count_before")
            attn2(T, T - 1)
            attn3(T, T - 1)
            attn4(T, T - 1)
            attn5(T, T - 1)
            attn6(T, T - 1)

            taken(dve, T, "count")
            chain(v.tensor_copy(tailrow[:, :], offs[0:1, :]))
            v.tensor_tensor(cnt[:, :], offs[0:1, :], region0[0:1, :], ALU.subtract).then_inc(sem("tails_known"), 1)
            dve.wait_ge(sem("tails_known"), 1)
            chain(v.tensor_scalar(tls[:, :], cnt[:, :], 1.0 / ROWS, 0.5 - 0.5 / ROWS, ALU.mult, ALU.add))
            chain(v.tensor_copy(tlsi[:, :], tls[:, :]))
            chain(v.tensor_copy(tls[:, :], tlsi[:, :]))
            chain(v.tensor_tensor_scan(tend[:, :], eones[:, :], tls[:, :], 0.0, ALU.mult, ALU.add))
            chain(v.tensor_tensor(tbeg[:, :], tend[:, :], tls[:, :], ALU.subtract))
            tile_i = bc(til[:, :], 2, E)
            chain(v.tensor_tensor(past[:, :, :], bc(tend[:, :], 1, MOE_TILES), tile_i, ALU.is_le))
            chain(v.tensor_reduce(tef[:, :], past[:, :, :], AX.X, ALU.add))
            chain(v.tensor_scalar(tex[:, 0:MOE_TILES], tef[:, :], float(E - 1), None, ALU.min))
            chain(v.tensor_copy(texi[:, :], tex[:, 0:2]))
            chain(v.tensor_tensor(ina[:, :, :], bc(tbeg[:, :], 1, MOE_TILES), tile_i, ALU.is_le))
            chain(v.tensor_tensor(ina[:, :, :], ina[:, :, :], past[:, :, :], ALU.subtract))
            chain(v.tensor_tensor(rowt[:, :, :], tile_i, bc(tbeg[:, :], 1, MOE_TILES), ALU.subtract))
            chain(v.tensor_scalar(rowt[:, :, :], rowt[:, :, :], float(ROWS), None, ALU.mult))
            chain(v.tensor_tensor(rowt[:, :, :], rowt[:, :, :], bc(region0[0:1, :], 1, MOE_TILES), ALU.add))
            chain(v.tensor_tensor(rowt[:, :, :], rowt[:, :, :], ina[:, :, :], ALU.mult))
            chain(v.tensor_reduce(trf[:, :], rowt[:, :, :], AX.X, ALU.add))
            chain(v.tensor_scalar(tef[:, :], tef[:, :], E - 0.5, float(E * REGION), ALU.is_gt, ALU.mult))
            v.tensor_tensor(firstrow[:, :], trf[:, :], tef[:, :], ALU.add).then_inc(sem("table_made"), 1)

            def inputs(r, u, e):
                i = UNROLL * r + u
                dve.wait_ge(sem("rows_turned"), i + 1)
                v.tensor_scalar(xeT[:, u % WBUFS, :], pG[u % 2][:, 0:ROWS], lngbT[:, bass.ds(e, 1)],
                                lngbT[:, bass.ds(e + E, 1)], ALU.mult, ALU.add).then_inc(sem("rows_scaled"), 1)
                v.tensor_copy(w1f[u % WBUFS][:, :], w1[:, bass.ds(e, 1), :].rearrange("p e f -> p (e f)")
                              ).then_inc(sem("inputs_ready"), 1)
                v.tensor_copy(w2f[u % WBUFS][:, :], w2[:, bass.ds(e, 1), :, :].rearrange("p e k c -> p (e k c)")
                              ).then_inc(sem("w2_copied"), 1)
                v.tensor_copy(b1f[:, u % WBUFS, :], b1T[:, :, bass.ds(e, 1)].rearrange("p k e -> p (k e)")
                              ).then_inc(sem("b1_copied"), 1)
                v.tensor_copy(b2f[:, u % WBUFS, :], b2p[:, bass.ds(e, 1), :].rearrange("p e c -> p (e c)")
                              ).then_inc(sem("weights_ready"), 1)

            def y_out(r, u):
                i = UNROLL * r + u
                dve.wait_ge(sem("result_ready"), i + 1)
                if not (isinstance(r, int) and r == 0 and u < OUTS):
                    dve.wait_ge(sem(f"y_sent{(u - OUTS) % UNROLL}"), 16 * SUBS * (r + (0 if u < OUTS else 1)))
                for j in range(SUBS):
                    v.tensor_scalar(yout[:, u % OUTS, j, :], pO[u % 2][:, C * j:C * j + C],
                                    xin[u // 4][:, u % 4, j, C:C + 1], None, ALU.mult
                                    ).then_inc(sem("y_weighted" if j == SUBS - 1 else "y_half"), 1)

            def round_(r, more):
                packed = dve.value_load(ahead[0:1, bass.ds(r, 1)], min_val=0, max_val=E ** UNROLL - 1)
                for u in range(UNROLL):
                    e = (packed >> (EBITS * u)) & (E - 1)
                    if u + 2 < UNROLL:
                        inputs(r, u + 2, e)
                    elif more:
                        inputs(r + 1, u + 2 - UNROLL, e)
                    if u > 0:
                        y_out(r, u - 1)
                    elif not (isinstance(r, int) and r == 0):
                        y_out(r - 1, UNROLL - 1)

            dve.wait_ge(sem("table_made"), 1)
            shifted = tex[:, 2:2 + MOE_TILES].rearrange("p (r u) -> p r u", u=UNROLL)
            chain(v.tensor_tensor(digits[:, :, :], shifted, bc(power[:, :], 1, ROUNDS), ALU.mult))
            chain(v.tensor_reduce(aheadf[:, :], digits[:, :, :], AX.X, ALU.add))
            v.tensor_copy(ahead[:, :], aheadf[:, :]).then_inc(sem("experts_packed"), 1)
            dve.wait_ge(sem("experts_packed"), 1)
            dve.wait_ge(sem("w1_loaded"), 16)
            dve.wait_ge(sem("w2_loaded"), 16 * E)
            for u in range(2):
                inputs(0, u, dve.value_load(texi[0:1, u:u + 1], min_val=0, max_val=E - 1))
            round_(0, True)
            with dve.Fori(1, ROUNDS - 1) as r:
                round_(r, True)
            round_(ROUNDS - 1, False)
            y_out(ROUNDS - 1, UNROLL - 1)

            for t in range(T):
                dve.wait_ge(sem(f"y_loaded{t}"), 16)
                v.tensor_tensor(x_tok[:, :, t, :], x_tok[:, :, t, :], ya[t][:, 0:B], ALU.add
                                ).then_inc(sem("sum_a"), 1)
                dve.wait_ge(sem("sum_a"), t + 1)
                v.tensor_tensor(x_tok[:, :, t, :], x_tok[:, :, t, :], ya[t][:, B:2 * B], ALU.add
                                ).then_inc(sem("sum_done"), 1)

        @block.gpsimd
        def _(pool):
            g = nc.gpsimd
            made = [0]

            def chain(ins):
                made[0] += 1
                ins.then_inc(sem("pool_chain"), 1)
                pool.wait_ge(sem("pool_chain"), made[0])

            def select(ap, pattern, op, fill, base, cm):
                return g.affine_select(ap, ap, pattern, op, fill, base, cm)

            chain(g.memset(ident[:, :], 0.0))
            select(ident[:, :], [[1, P]], ALU.not_equal, 1.0, 0, -1).then_inc(sem("ident_made"), 1)
            chain(g.memset(block4[:, :], 1.0))
            chain(select(block4[:, :], [[-4, 32], [0, 4]], ALU.is_ge, 0.0, 0, 1))
            chain(select(block4[:, :], [[4, 32], [0, 4]], ALU.is_ge, 0.0, 3, -1))
            g.tensor_scalar(avg4[:, :], block4[:, :], 0.25, 0.0, ALU.mult, ALU.add).then_inc(sem("block4_made"), 1)
            pool.wait_ge(sem("ident_made"), 1)
            chain(g.tensor_copy(ident_b[:, :], ident[:, :]))
            chain(g.memset(maskneg[:, :, :], 0.0))
            chain(select(maskneg[:, :, :], [[0, B], [1, P]], ALU.is_ge, NEG, 0, -1))
            chain(g.memset(ones_b[:, :], 1.0))
            chain(g.memset(before[:, :], 1.0))
            chain(select(before[:, :], [[1, P]], ALU.is_ge, 0.0, -1, -1))
            chain(g.memset(headmask[:, :, :], 1.0))
            hm = headmask[:, :, :]
            chain(select(hm, [[-DH, HPH], [0, DE]], ALU.is_ge, 0.0, 0, 1))
            chain(select(hm, [[DH, HPH], [0, DE]], ALU.is_ge, 0.0, DH - 1, -1))
            chain(g.memset(pick[:, :, :], 0.0))
            for k in range(3):
                chain(select(pick[BH * k:BH * k + BH, :, :], [[1, NH], [NH, B]], ALU.not_equal, 1.0, 0, -1))
            chain(g.memset(spread[:, :, :, :, :], 0.0))
            for f in range(HALVES):
                chain(select(spread[:, f], [[NH, B], [1, HPH], [0, DH]], ALU.not_equal, 1.0, HPH * f, -1))
            chain(g.tensor_tensor(hsum[:, :], pick[:, :, 0], pick[:, :, 1], ALU.add))
            chain(g.tensor_tensor(hsum[:, :], hsum[:, :], pick[:, :, 2], ALU.add))
            chain(g.tensor_tensor(hsum[:, :], hsum[:, :], pick[:, :, 3], ALU.add))
            chain(g.tensor_scalar(neghead[:, :], hsum[:, :], -1.0, 0.0, ALU.mult, ALU.add))
            chain(g.tensor_tensor(ofbatch[:, :], pick[:, 0, :], pick[:, 1, :], ALU.add))
            for h in range(2, NH):
                chain(g.tensor_tensor(ofbatch[:, :], ofbatch[:, :], pick[:, h, :], ALU.add))
            chain(g.memset(lower8[:, :, :], 1.0))
            chain(select(lower8[:, :, :], [[1, E], [-1, E]], ALU.is_ge, 0.0, -1, 0))
            chain(g.memset(causal4[:, :, :], 1.0))
            chain(select(causal4[:, :, :], [[1, B], [-1, B]], ALU.is_ge, 0.0, 0, 0))
            chain(g.iota(iota8[:, :], [[REGION, E]], 0, 0))
            chain(g.tensor_copy(region0[:, :], iota8[:, :]))
            chain(g.iota(iota8[:, :], [[S, B], [TOK, 2]], 0, 1))
            chain(g.tensor_copy(dest[:, :, :].rearrange("p b k -> p (b k)"), iota8[:, :]))
            chain(g.iota(iotat[:, :], [[1, MOE_TILES]], 0, 0))
            chain(g.tensor_copy(til[:, :], iotat[:, :]))
            for u in range(UNROLL):
                chain(g.memset(power[:, u:u + 1], float(E ** u)))
            chain(g.memset(tex[:, MOE_TILES:MOE_TILES + 2], 0.0))
            chain(g.memset(tail[:, :], 0.0))
            chain(g.iota(tail[:, C + 1:C + 2].bitcast(I32), [[0, 1]], SKIP, 0))
            g.memset(tail[:, C:C + 1], 0.0).then_inc(sem("pool_tables_made"), 1)
            taken(pool, None, "gvar")
            g.tensor_tensor(gr[:, :], gr[:, :], mhalf[:, 0:B], ALU.pow).then_inc(sem("gr_done"), 1)

            def values_scaled(t):
                w = gtok[:, 0].rearrange("p b h -> p (b h)")
                g.tensor_tensor(vs[:, :, :, :].rearrange("p b h d -> p (b h) d"),
                                vext[:, :, :, :].rearrange("p b h d -> p (b h) d"), bc(w, 2, DE), ALU.mult
                                ).then_inc(sem("vs_ready"), 1)

            def square(t, f):
                pool.wait_ge(sem("norm_read"), 2 * t + f + 1)
                g.tensor_tensor(dsq[:, f].rearrange("p b h d -> p (b h d)"), dd[:, f].rearrange("p b h d -> p (b h d)"),
                                dd[:, f].rearrange("p b h d -> p (b h d)"), ALU.mult).then_inc(sem("dsq_done"), 1)

            def rsqrt(ap, n, ready, count, done):
                pool.wait_ge(sem(ready), count)
                g.tensor_tensor(ap, ap, mhalf[:, 0:n], ALU.pow).then_inc(sem(done), 1)

            def scatter(s):
                wait_apart(pool, sem("slots_ready"), s + 1)
                wait_apart(pool, sem("row_part"), (2 + B) * (s + 1))
                for k in range(2):
                    for b in range(B):
                        g.indirect_dma_start(
                            xs, bass.IndirectOffsetOnAxis(slot[:, k, b:b + 1].bitcast(U32), 0), xrow[:, b, k, :], None
                        ).then_inc(sem(f"scattered{k}{b}"), 16)

            def late(s):
                rsqrt(rs3[:, :], B, "var3_ready", s + 1, "rs3_ready")

            def late2(s):
                pool.wait_ge(sem("v2_ready"), s + 1)
                g.tensor_tensor(rs4[:, :], v2[:, :], mhalf[:, 0:B], ALU.pow).then_inc(sem("rs4_ready"), 1)

            def head_rstd(t, f):
                rsqrt(var[:, f].rearrange("p b h -> p (b h)"), B * HPH, "var_c", 2 * t + f + 1, "rstd_ready")

            def row_rstd(s):
                rsqrt(rs1[:, :], B, "var1_ready", s + 1, "rs1_ready")

            def step(t):
                first, last = (isinstance(t, int) and t == 0), (isinstance(t, int) and t == T - 1)
                if not last:
                    pool.wait_ge(sem("gscale_ready"), t + 1)
                    values_scaled(t)
                wait_apart(pool, sem("xact_ready"), 2 * t + 2)
                if not first:
                    wait_apart(pool, sem("y_ready"), 2 * t)
                for f in range(HALVES):
                    g.tensor_scalar(sx[:, f], xact[:, f], vecs[:, 2, f:f + 1], 0.0, ALU.mult, ALU.add
                                    ).then_inc(sem("sx_ready" if f else "sx_half"), 1)
                if not first:
                    row_rstd(t - 1)
                square(t, 0)
                head_rstd(t, 0)
                if not last:
                    pool.wait_ge(sem("state_taken"), B * HALVES * (t + 1))
                    g.tensor_tensor(KVm[:, :, :], KV[:, :, :],
                                    bc(headmask[:, :, :].rearrange("p h d -> p (h d)"), 1, HALVES * B),
                                    ALU.mult).then_inc(sem("state_ready"), 1)
                square(t, 1)
                if not first:
                    late(t - 1)
                if last:
                    head_rstd(t, 1)
                    late2(t - 1)
                    return
                if not first:
                    late2(t - 1)
                head_rstd(t, 1)
                if not first:
                    scatter(t - 1)

            between(pool, step)
            row_rstd(T - 1)
            late(T - 1)
            scatter(T - 2)
            late2(T - 1)
            scatter(T - 1)

            def send(r, u):
                wait_apart(pool, sem("y_weighted"), UNROLL * r + u + 1)
                for j in range(SUBS):
                    g.indirect_dma_start(
                        y2, bass.IndirectOffsetOnAxis(xin[u // 4][:, u % 4, j, C + 1:C + 2].bitcast(U32), 0),
                        yout[:, u % OUTS, j, :], None, bounds_check=2 * TOK - 1, oob_is_err=False
                    ).then_inc(sem(f"y_sent{u}"), 16)

            for u in range(UNROLL):
                send(0, u)
            with pool.Fori(1, ROUNDS) as r:
                for u in range(UNROLL):
                    send(r, u)


_INS = ['x', 'L0_conv_W_up', 'L0_conv_conv_w', 'L0_conv_conv_b', 'L0_conv_Wq', 'L0_conv_Wk', 'L0_conv_Wv',
        'L0_conv_W_i', 'L0_conv_b_i', 'L0_conv_W_f', 'L0_conv_b_f', 'L0_conv_norm_w', 'L0_conv_skip',
        'L0_conv_W_down', 'L1_attn_fc_w', 'L1_attn_fc_b', 'L1_attn_score_w', 'L1_ffn_Wr', 'L1_ffn_br',
        'L1_ffn_ln_g', 'L1_ffn_ln_b', 'L1_ffn_W1', 'L1_ffn_b1', 'L1_ffn_W2', 'L1_ffn_b2']


def kernel(**inputs):
    import numpy as _np
    import concourse.bacc as _bacc
    from concourse import mybir as _mybir
    from concourse.bass_utils import run_bass_kernel_spmd as _run

    nc = _bacc.Bacc("TRN2", target_bir_lowering=False, num_devices=1)
    arrays, args = {}, {}
    for name in _INS:
        arr = _np.ascontiguousarray(inputs[name])
        arrays[f"in_{name}"] = arr
        args[name] = nc.dram_tensor(f"in_{name}", arr.shape, _mybir.dt.from_np(arr.dtype), kind="ExternalInput").ap()
    out = nc.dram_tensor("out_0", (B, 32, 32, C), _mybir.dt.float32, kind="ExternalOutput").ap()
    block_kernel(nc, args, out)
    r = _run(nc, [arrays], core_ids=[0])
    return r.results[0]["out_0"]
```
